# Optimizing a Trainium2 kernel written in Bass

```python
import numpy as np
import jax
import jax.numpy as jnp

def _softmax(x, axis=-1):
    return jax.nn.softmax(x, axis=axis)

def _gelu(x):
    return jax.nn.gelu(x, approximate=True)

def _silu(x):
    return jax.nn.silu(x)

def _sigmoid(x):
    return jax.nn.sigmoid(x)

def _layernorm(x, axis=-1, eps=1e-05):
    m = jnp.mean(x, axis=axis, keepdims=True)
    v = jnp.var(x, axis=axis, keepdims=True)
    return (x - m) / jnp.sqrt(v + eps)

def _scatter_add(tgt, idx, src, axis=0):
    return tgt.at[idx].add(src)

def _segment_sum(src, seg, n):
    return jax.ops.segment_sum(src, seg, n)
kernel_name = 'mk_vit_tower_d1_tok_img512_r4_c966cf'

def setup_inputs(seed: int=0):
    np.random.seed(seed)
    _w = jnp.asarray

    def _rec_inputs():
        import jax
        import jax.numpy as jnp
        _rk = jax.random.key(seed)
        x = -0.000147625 + 0.999875 * jax.random.normal(jax.random.fold_in(_rk, 1), (64, 3, 224, 224), jnp.float32)
        return x
    x = _rec_inputs()

    def _L0_tok_setup():
        import jax, jax.numpy as jnp
        import numpy as np
        N_PATCHES = 8
        PATCH = 28
        C = 3
        IN_D = C * PATCH * PATCH
        HID = 128
        SEQ = N_PATCHES * N_PATCHES + 1

        def _positional_embedding(seq_len, dim):
            i = np.arange(seq_len)[:, None].astype(np.float32)
            j = np.arange(dim)[None, :].astype(np.float32)
            ang = i / np.power(100000.0, j / dim)
            pe = np.where(j % 2 == 0, np.sin(ang), np.cos(ang))
            return jnp.asarray(pe, dtype=jnp.float32)
        key = jax.random.key(seed)
        k1, k2, k3, k4 = jax.random.split(key, 4)
        B = 64
        X = jax.random.normal(k1, (B, C, 224, 224), dtype=jnp.float32)
        bound = 1.0 / np.sqrt(IN_D)
        W = jax.random.uniform(k2, (HID, IN_D), minval=-bound, maxval=bound, dtype=jnp.float32)
        b = jax.random.uniform(k3, (HID,), minval=-bound, maxval=bound, dtype=jnp.float32)
        class_token = jax.random.uniform(k4, (1, HID), dtype=jnp.float32)
        pos_embed = _positional_embedding(SEQ, HID)
        return {'X': X, 'W': W, 'b': b, 'class_token': class_token, 'pos_embed': pos_embed}
    _L0_tok_all = _L0_tok_setup()
    _L0_tok_in = {k: v for k, v in _L0_tok_all.items() if k in ('W', 'b', 'class_token', 'pos_embed')}
    del _L0_tok_all

    def _L0_attn_setup():
        import jax, jax.numpy as jnp
        import numpy as np
        D_MODEL = 128
        N_HEADS = 8
        D_HEAD = D_MODEL // N_HEADS
        EPS = 1e-06

        def _split_heads(t, B, S):
            return t.reshape(B, S, N_HEADS, D_HEAD).transpose(0, 2, 1, 3)

        def _reference_tuple_inner(x, Wq, bq, Wk, bk, Wv, bv, Wo, bo):
            B, S, _ = x.shape
            q = _split_heads(x @ Wq.T + bq, B, S)
            k = _split_heads(x @ Wk.T + bk, B, S)
            v = _split_heads(x @ Wv.T + bv, B, S)
            q = jax.nn.relu(q)
            k = jax.nn.relu(k)
            k_sum = k.sum(axis=-1, keepdims=True)
            attn = jnp.einsum('bhnd,bhmd->bhnm', q, k) / (k_sum + EPS)
            attn = jax.nn.softmax(attn, axis=-1)
            out = jnp.einsum('bhnm,bhmd->bhnd', attn, v)
            out = out.transpose(0, 2, 1, 3).reshape(B, S, D_MODEL)
            return (out @ Wo.T + bo, attn)
        key = jax.random.key(seed)
        ks = jax.random.split(key, 9)
        B, S = (2, 512)
        scale = 0.02
        x = jax.random.normal(ks[0], (B, S, D_MODEL), dtype=jnp.float32)
        Wq = jax.random.normal(ks[1], (D_MODEL, D_MODEL), dtype=jnp.float32) * scale
        Wk = jax.random.normal(ks[2], (D_MODEL, D_MODEL), dtype=jnp.float32) * scale
        Wv = jax.random.normal(ks[3], (D_MODEL, D_MODEL), dtype=jnp.float32) * scale
        Wo = jax.random.normal(ks[4], (D_MODEL, D_MODEL), dtype=jnp.float32) * scale
        bq = jax.random.normal(ks[5], (D_MODEL,), dtype=jnp.float32) * scale
        bk = jax.random.normal(ks[6], (D_MODEL,), dtype=jnp.float32) * scale
        bv = jax.random.normal(ks[7], (D_MODEL,), dtype=jnp.float32) * scale
        bo = jax.random.normal(ks[8], (D_MODEL,), dtype=jnp.float32) * scale
        return {'x': x, 'Wq': Wq, 'bq': bq, 'Wk': Wk, 'bk': bk, 'Wv': Wv, 'bv': bv, 'Wo': Wo, 'bo': bo}
    _L0_attn_all = _L0_attn_setup()
    _L0_attn_in = {k: v for k, v in _L0_attn_all.items() if k in ('Wq', 'bq', 'Wk', 'bk', 'Wv', 'bv', 'Wo', 'bo')}
    del _L0_attn_all

    def _L0_ffn_setup():
        import jax, jax.numpy as jnp
        import numpy as np
        B, T, C = (8, 256, 128)
        H = 256
        G, EG = (2, 4)
        E = G * EG
        K = 2
        LN_EPS = 1e-05

        def _swiglu(x):
            a, b = jnp.split(x, 2, axis=-1)
            return jax.nn.silu(a) * b
        key = jax.random.key(seed)
        ks = jax.random.split(key, 8)
        n = lambda k, shape, s: jax.random.normal(k, shape, dtype=jnp.float32) * s
        return {'x': n(ks[0], (B, T, C), 1.0), 'ln_scale': jnp.ones((C,), jnp.float32), 'ln_bias': jnp.zeros((C,), jnp.float32), 'shared_in_w': n(ks[1], (2 * H, C), 0.02), 'shared_out_w': n(ks[2], (C, H), 0.02), 'shared_out_b': jnp.zeros((C,), jnp.float32), 'expert_in_w': n(ks[3], (2 * H, C), 0.02), 'expert_out_weight': n(ks[4], (E, C, H), 0.02), 'expert_out_bias': jnp.zeros((E, C), jnp.float32), 'group_gate_w': n(ks[5], (G, C), 0.02), 'expert_gate_w': n(ks[6], (E, C), 0.02), 'group_bias': jnp.zeros((G,), jnp.float32), 'expert_bias': jnp.zeros((E,), jnp.float32)}
    _L0_ffn_all = _L0_ffn_setup()
    _L0_ffn_in = {k: v for k, v in _L0_ffn_all.items() if k in ('ln_scale', 'ln_bias', 'shared_in_w', 'shared_out_w', 'shared_out_b', 'expert_in_w', 'expert_out_weight', 'expert_out_bias', 'group_gate_w', 'expert_gate_w', 'group_bias', 'expert_bias')}
    del _L0_ffn_all
    return {'x': x, 'L0_tok_W': _L0_tok_in['W'], 'L0_tok_b': _L0_tok_in['b'], 'L0_tok_class_token': _L0_tok_in['class_token'], 'L0_tok_pos_embed': _L0_tok_in['pos_embed'], 'L0_attn_Wq': _L0_attn_in['Wq'], 'L0_attn_bq': _L0_attn_in['bq'], 'L0_attn_Wk': _L0_attn_in['Wk'], 'L0_attn_bk': _L0_attn_in['bk'], 'L0_attn_Wv': _L0_attn_in['Wv'], 'L0_attn_bv': _L0_attn_in['bv'], 'L0_attn_Wo': _L0_attn_in['Wo'], 'L0_attn_bo': _L0_attn_in['bo'], 'L0_ffn_ln_scale': _L0_ffn_in['ln_scale'], 'L0_ffn_ln_bias': _L0_ffn_in['ln_bias'], 'L0_ffn_shared_in_w': _L0_ffn_in['shared_in_w'], 'L0_ffn_shared_out_w': _L0_ffn_in['shared_out_w'], 'L0_ffn_shared_out_b': _L0_ffn_in['shared_out_b'], 'L0_ffn_expert_in_w': _L0_ffn_in['expert_in_w'], 'L0_ffn_expert_out_weight': _L0_ffn_in['expert_out_weight'], 'L0_ffn_expert_out_bias': _L0_ffn_in['expert_out_bias'], 'L0_ffn_group_gate_w': _L0_ffn_in['group_gate_w'], 'L0_ffn_expert_gate_w': _L0_ffn_in['expert_gate_w'], 'L0_ffn_group_bias': _L0_ffn_in['group_bias'], 'L0_ffn_expert_bias': _L0_ffn_in['expert_bias']}

def reference(x, L0_tok_W, L0_tok_b, L0_tok_class_token, L0_tok_pos_embed, L0_attn_Wq, L0_attn_bq, L0_attn_Wk, L0_attn_bk, L0_attn_Wv, L0_attn_bv, L0_attn_Wo, L0_attn_bo, L0_ffn_ln_scale, L0_ffn_ln_bias, L0_ffn_shared_in_w, L0_ffn_shared_out_w, L0_ffn_shared_out_b, L0_ffn_expert_in_w, L0_ffn_expert_out_weight, L0_ffn_expert_out_bias, L0_ffn_group_gate_w, L0_ffn_expert_gate_w, L0_ffn_group_bias, L0_ffn_expert_bias):
    import jax
    import jax.numpy as jnp

    def _L0_tok_ref(X, W, b, class_token, pos_embed):
        import jax, jax.numpy as jnp
        import numpy as np
        N_PATCHES = 8
        PATCH = 28
        C = 3
        IN_D = C * PATCH * PATCH
        HID = 128
        SEQ = N_PATCHES * N_PATCHES + 1

        def _positional_embedding(seq_len, dim):
            i = np.arange(seq_len)[:, None].astype(np.float32)
            j = np.arange(dim)[None, :].astype(np.float32)
            ang = i / np.power(100000.0, j / dim)
            pe = np.where(j % 2 == 0, np.sin(ang), np.cos(ang))
            return jnp.asarray(pe, dtype=jnp.float32)
        B = X.shape[0]
        patches = X.reshape(B, C, N_PATCHES, PATCH, N_PATCHES, PATCH)
        patches = patches.transpose(0, 2, 4, 1, 3, 5).reshape(B, N_PATCHES * N_PATCHES, IN_D)
        tokens = jnp.einsum('bpi,hi->bph', patches, W) + b
        cls = jnp.broadcast_to(class_token[None, :, :], (B, 1, HID))
        tokens = jnp.concatenate([cls, tokens], axis=1)
        return tokens * pos_embed[None, :, :]

    def _L0_attn_ref(x, Wq, bq, Wk, bk, Wv, bv, Wo, bo):
        import jax, jax.numpy as jnp
        import numpy as np
        D_MODEL = 128
        N_HEADS = 8
        D_HEAD = D_MODEL // N_HEADS
        EPS = 1e-06

        def _split_heads(t, B, S):
            return t.reshape(B, S, N_HEADS, D_HEAD).transpose(0, 2, 1, 3)

        def _reference_tuple_inner(x, Wq, bq, Wk, bk, Wv, bv, Wo, bo):
            B, S, _ = x.shape
            q = _split_heads(x @ Wq.T + bq, B, S)
            k = _split_heads(x @ Wk.T + bk, B, S)
            v = _split_heads(x @ Wv.T + bv, B, S)
            q = jax.nn.relu(q)
            k = jax.nn.relu(k)
            k_sum = k.sum(axis=-1, keepdims=True)
            attn = jnp.einsum('bhnd,bhmd->bhnm', q, k) / (k_sum + EPS)
            attn = jax.nn.softmax(attn, axis=-1)
            out = jnp.einsum('bhnm,bhmd->bhnd', attn, v)
            out = out.transpose(0, 2, 1, 3).reshape(B, S, D_MODEL)
            return (out @ Wo.T + bo, attn)
        return _reference_tuple_inner(x, Wq, bq, Wk, bk, Wv, bv, Wo, bo)[0]

    def _L0_ffn_ref(x, ln_scale, ln_bias, shared_in_w, shared_out_w, shared_out_b, expert_in_w, expert_out_weight, expert_out_bias, group_gate_w, expert_gate_w, group_bias, expert_bias):
        import jax, jax.numpy as jnp
        import numpy as np
        B, T, C = (8, 256, 128)
        H = 256
        G, EG = (2, 4)
        E = G * EG
        K = 2
        LN_EPS = 1e-05

        def _swiglu(x):
            a, b = jnp.split(x, 2, axis=-1)
            return jax.nn.silu(a) * b
        Bx, Tx, Cx = x.shape
        S = Bx * Tx
        flat = x.reshape(S, Cx)
        mu = flat.mean(-1, keepdims=True)
        var = ((flat - mu) ** 2).mean(-1, keepdims=True)
        flat = (flat - mu) * jax.lax.rsqrt(var + LN_EPS) * ln_scale + ln_bias
        h_shared = _swiglu(flat @ shared_in_w.T)
        out_shared = h_shared @ shared_out_w.T + shared_out_b
        g_logits = flat @ group_gate_w.T + group_bias
        g_idx = jnp.argmax(g_logits, axis=-1)
        e_logits = (flat @ expert_gate_w.T).reshape(S, G, EG)
        e_sel = jnp.take_along_axis(e_logits, g_idx[:, None, None], axis=1)[:, 0, :]
        e_sel = e_sel + expert_bias.reshape(G, EG)[g_idx]
        e_probs = jax.nn.softmax(e_sel, axis=-1)
        topv, topi = jax.lax.top_k(e_probs, K)
        topv = topv / (topv.sum(-1, keepdims=True) + 1e-08)
        disp = g_idx[:, None] * EG + topi
        h_expert = _swiglu(flat @ expert_in_w.T)
        rows = jnp.arange(S)[:, None]
        comb = jnp.zeros((S, E), flat.dtype).at[rows, disp].add(topv)
        cnt = jnp.zeros((S, E), flat.dtype).at[rows, disp].add(1.0)
        routed = cnt @ expert_out_bias
        for e in range(E):
            routed = routed + comb[:, e:e + 1] * (h_expert @ expert_out_weight[e].T)
        return (out_shared + routed).reshape(Bx, Tx, Cx)
    h = _L0_tok_ref(x, L0_tok_W, L0_tok_b, L0_tok_class_token, L0_tok_pos_embed)
    h = h + _L0_attn_ref(_layernorm(h, axis=-1), L0_attn_Wq, L0_attn_bq, L0_attn_Wk, L0_attn_bk, L0_attn_Wv, L0_attn_bv, L0_attn_Wo, L0_attn_bo)
    h = h + _L0_ffn_ref(_layernorm(h, axis=-1), L0_ffn_ln_scale, L0_ffn_ln_bias, L0_ffn_shared_in_w, L0_ffn_shared_out_w, L0_ffn_shared_out_b, L0_ffn_expert_in_w, L0_ffn_expert_out_weight, L0_ffn_expert_out_bias, L0_ffn_group_gate_w, L0_ffn_expert_gate_w, L0_ffn_group_bias, L0_ffn_expert_bias)
    return h

_drawn_inputs = setup_inputs


def setup_inputs(seed=0):
    import zlib

    import numpy as np

    out = dict(_drawn_inputs(seed))
    spreads = {'L0_ffn_ln_scale': (1.0, 0.2),
     'L0_ffn_ln_bias': (0.0, 0.1),
     'L0_ffn_shared_out_b': (0.0, 0.1),
     'L0_ffn_expert_out_bias': (0.0, 0.1),
     'L0_ffn_group_bias': (0.0, 0.1),
     'L0_ffn_expert_bias': (0.0, 0.1)}
    factors = {'L0_attn_Wq': 4.228,
     'L0_attn_bq': 7.216,
     'L0_attn_Wk': 3.932,
     'L0_attn_bk': 25.755,
     'L0_ffn_shared_in_w': 2.724,
     'L0_ffn_shared_out_w': 2.737,
     'L0_ffn_expert_in_w': 3.761,
     'L0_ffn_expert_out_weight': 3.749}
    for name, (base, spread) in spreads.items():
        noise = np.random.default_rng([zlib.crc32(name.encode()), seed]).standard_normal(out[name].shape)
        drawn = base * np.exp(spread * noise) if base else spread * noise
        out[name] = jnp.asarray(drawn.astype(out[name].dtype))
    for name, factor in factors.items():
        out[name] = (out[name] * factor).astype(out[name].dtype)
    return out
```

```python
from contextlib import ExitStack

import numpy as np
import concourse.bass as bass
from concourse import mybir

F32 = mybir.dt.float32
F32R = mybir.dt.float32r
ALU = mybir.AluOpType
ACT = mybir.ActivationFunctionType
AX = mybir.AxisListType

IMAGES, CHANNELS, SIDE, GRID = 64, 3, 224, 8
PATCH = SIDE // GRID
NPATCH = GRID * GRID
SEQ = NPATCH + 1
D = 128
IN_D = CHANNELS * PATCH * PATCH
NMAIN = IN_D // 128
NTAIL = IN_D - NMAIN * 128
GROUP_IMAGES = 8
GROUPS = IMAGES // GROUP_IMAGES
TOK = GROUP_IMAGES * NPATCH
TILES = TOK // 128
HEADS, DH = 8, 16
HP = HEADS // 2
H = 256
HC = H // 128
EXPERTS, EG = 8, 4
NGATE = 2 + EXPERTS
ATTN_EPS = 1e-6
LN_EPS = 1e-5
PIECES = [(j, j + 3) for j in range(0, NMAIN, 3)]

C_ID, C_PAR, C_TRI, C_THR, C_HROW, C_HMASK, C_PMASK = 0, 128, 130, 146, 150, 158, 286
C_B2, C_HEAD = 302, 304
NCONST = 312


def shape_constants():
    c = np.zeros((128, NCONST), np.float32)
    p = np.arange(128)
    c[:, C_ID:C_ID + 128] = np.eye(128)
    c[:, C_PAR:C_PAR + 2] = (p[:, None] // DH % 2) == np.arange(2)
    i, j = np.meshgrid(np.arange(EG), np.arange(EG), indexing="ij")
    c[:, C_TRI:C_TRI + 16] = (j < i).reshape(1, 16)
    c[:, C_THR:C_THR + EG] = np.arange(EG)[None] - 1
    c[:, C_HROW:C_HROW + 8] = (p[:, None] % 8) == np.arange(8)
    c[:, C_HMASK:C_HMASK + 128] = (p[:, None] % 8) == (np.arange(128)[None] // DH)
    c[:, C_PMASK:C_PMASK + 16] = (p[:, None] // 8) == np.arange(16)
    c[:, C_B2:C_B2 + 2] = (p[:, None] // 64) == np.arange(2)
    c[:, C_HEAD:C_HEAD + HEADS] = (p[:, None] // DH) == np.arange(HEADS)
    return c


class Event:

    def __init__(self, ctx, nc, name, per=1):
        self.sem = ctx.enter_context(nc.semaphore(name))
        self.per = per


def need(engine, event, g, k=None):
    value = event.per * g + (event.per if k is None else k)
    if isinstance(value, int) and value <= 0:
        return
    engine.wait_ge(event.sem, value)


def vit_tower(nc, A, out):
    ctx = ExitStack()
    with ctx:
        def sb(name, shape, dt=F32):
            return ctx.enter_context(nc.sbuf_tensor(name, shape, dt))

        def ps(name, shape):
            return ctx.enter_context(nc.psum_tensor(name, shape, F32))

        def ev(name, per=1):
            return Event(ctx, nc, name, per)

        const = sb("const", [128, NCONST])
        w_patch = sb("w_patch", [128, NMAIN, D])
        w_patch_tail = sb("w_patch_tail", [NTAIL, D])
        tok_b = sb("tok_b", [128, 1])
        pos_t = sb("pos_t", [128, NPATCH])
        wq = sb("wq", [128, D])
        wk = sb("wk", [128, D])
        wv = sb("wv", [128, D])
        wo = sb("wo", [128, D])
        bk_col = sb("bk_col", [128, 1])
        bv_col = sb("bv_col", [128, 1])
        bq_row = sb("bq_row", [128, D])
        ln_scale = sb("ln_scale", [128, 1])
        ln_bias = sb("ln_bias", [128, 1])
        w_in_lo = sb("w_in_lo", [128, 2, 2 * H], F32R)
        w_in_hi = sb("w_in_hi", [128, 2, 2 * H], F32R)
        w_gate = sb("w_gate", [128, NGATE])
        gate_b = sb("gate_b", [128, NGATE])
        w_sout = sb("w_sout", [128, HC, D])
        w_eout_lo = sb("w_eout_lo", [128, HC, EXPERTS, D], F32R)
        w_eout_hi = sb("w_eout_hi", [128, HC, EXPERTS, D], F32R)
        out_bias = sb("out_bias", [EXPERTS + 1, D])

        ident = const[:, C_ID:C_ID + 128]

        x_main = sb("x_main", [128, NMAIN, TOK])
        x_tail = sb("x_tail", [NTAIL, TOK])
        h_t = sb("h_t", [128, TOK])
        h_nat = [sb(f"h_nat{i}", [128, TOK]) for i in range(2)]
        stats1 = sb("stats1", [128, TILES, 6])
        mv1 = sb("mv1", [128, 6, TILES])
        var1 = sb("var1", [128, TILES])
        rstd1 = sb("rstd1", [128, TILES])
        neg_half = sb("neg_half", [128, TILES])
        hn_nat = sb("hn_nat", [128, TOK])
        hn_t = sb("hn_t", [128, TOK])
        q_mask = sb("q_mask", [128, GROUP_IMAGES, 2, NPATCH])
        k_t = sb("k_t", [128, TOK])
        k_sel = sb("k_sel", [128, 2 * HEADS])
        q_sum_eps = sb("q_sum_eps", [128, TILES, HEADS])
        q_rec = sb("q_rec", [128, TILES, HEADS])
        q_nat = sb("q_nat", [128, TOK])
        k_bd = sb("k_bd", [128, GROUP_IMAGES, HP, SEQ])
        v_bd = sb("v_bd", [128, IMAGES // 2, HP, 2, 32])
        shift = [sb(f"shift{i}", [128, 2, HP, SEQ]) for i in range(2)]
        probs = [sb(f"probs{i}", [128, HP, 2 * NPATCH]) for i in range(2)]
        exp_cls = sb("exp_cls", [128, TILES, HP, 2])
        patch_sum = sb("patch_sum", [128, TILES, HP, 2])
        row_max = [sb(f"row_max{i}", [128, 2, HP]) for i in range(2)]
        row_sum = sb("row_sum", [128, TILES, HP, 2])
        row_rec = sb("row_rec", [128, TILES, HP, 2])
        probs_t = [sb(f"probs_t{i}", [128, 512]) for i in range(2)]
        attn_patch = [sb(f"attn_patch{i}", [128, 8, 2, DH]) for i in range(2)]
        p_cls = [sb(f"p_cls{i}", [128, 2, HP, 2]) for i in range(2)]
        attn_cls = [sb(f"attn_cls{i}", [128, 2, HP, 2, DH]) for i in range(2)]
        attn_nat = sb("attn_nat", [128, TILES, HP, 2, DH])
        attn_t = sb("attn_t", [128, TOK])
        h2 = [sb(f"h2_{i}", [128, TOK]) for i in range(2)]
        stats2 = sb("stats2", [128, TILES, 6])
        mv2 = sb("mv2", [128, 6, TILES])
        var2 = sb("var2", [128, TILES])
        rstd2 = sb("rstd2", [128, TILES])
        z_nat = sb("z_nat", [128, TOK])
        z_t = sb("z_t", [128, TOK])
        z_hi = sb("z_hi", [128, TOK], F32R)
        z_lo = sb("z_lo", [128, TOK], F32R)
        cls_scores = sb("cls_scores", [128, IMAGES // 2 * HEADS])
        g_logit = sb("g_logit", [128, TILES, 2])
        e_logit = sb("e_logit", [128, TILES * 2, EG])
        g_sel = sb("g_sel", [128, TILES, 2])
        e_max = sb("e_max", [128, TILES * 2])
        e_shift = sb("e_shift", [128, TILES * 2, EG])
        e_exp = sb("e_exp", [128, TILES * 2, EG])
        e_ge = sb("e_ge", [128, TILES * 2, EG * EG])
        e_row = sb("e_row", [128, TILES * 2, EG])
        e_col = sb("e_col", [128, TILES * 2, EG])
        e_top = sb("e_top", [128, TILES * 2, EG])
        count = sb("count", [128, TILES, EXPERTS + 1])
        e_keep = sb("e_keep", [128, TILES, EXPERTS])
        e_group = sb("e_group", [128, TILES, EXPERTS])
        e_den = sb("e_den", [128, 4, TILES])
        comb = sb("comb", [128, TILES, EXPERTS])
        count_t = sb("count_t", [EXPERTS + 1, TOK])
        silu = [sb(f"silu{i}", [128, TOK]) for i in range(2)]
        hidden = sb("hidden", [128, HC, TOK])
        hidden_hi = sb("hidden_hi", [128, HC, TOK], F32R)
        hidden_lo = sb("hidden_lo", [128, HC, TOK], F32R)
        prod = [sb(f"prod{i}", [128, 2, EG * D]) for i in range(2)]
        routed = sb("routed", [128, TILES, D])
        y_out = sb("y_out", [128, TOK])
        free = [b[:, i * D:(i + 1) * D] for b in (hidden[:, 0], hidden[:, 1], y_out, routed.rearrange("p t d -> p (t d)"))
                for i in range(4)]
        (bk_row, bo_row, cls_row, pos0_row, h_cls, hn_cls, hn_cls_t, q_cls_raw, q_cls, k_cls_raw, k_cls, qn_cls, v_cls,
         cc_mul) = free[:14]
        w_in_raw, w_eout_raw = silu, prod
        cls_stats = sb("cls_stats", [128, 6])
        cls_mv = sb("cls_mv", [128, 2])
        cls_var = sb("cls_var", [128, 1])
        cls_rstd = sb("cls_rstd", [128, 1])
        k_cls_sum = sb("k_cls_sum", [128, 3 * HEADS])
        k_cls_t = sb("k_cls_t", [128, 1])
        qn_cls_t = sb("qn_cls_t", [128, 1])
        v_cls_hp = sb("v_cls_hp", [128, HP, DH])
        bo2 = sb("bo2", [128, D])
        cc_row = sb("cc_row", [128, HEADS])
        cc_pick = sb("cc_pick", [128, HEADS])
        cc_col = sb("cc_col", [128, 1])
        v_cls_rows = sb("v_cls_rows", [128, D])
        h_cls_bo = sb("h_cls_bo", [128, D])
        tc_max0 = sb("tc_max0", [128, 4])
        tc_max = sb("tc_max", [128, 4])
        tc_shift = x_main[:, 8, 0:4 * NPATCH].rearrange("p (a m) -> p a m", m=NPATCH)
        tc_exp = x_main[:, 9, 0:4 * NPATCH].rearrange("p (a m) -> p a m", m=NPATCH)
        tc_cc = sb("tc_cc", [128, 4])
        tc_cc_exp = sb("tc_cc_exp", [128, 4])
        tc_sum = sb("tc_sum", [128, 3, 4])
        tc_prob = x_main[:, 10, 0:4 * NPATCH].rearrange("p (a m) -> p a m", m=NPATCH)
        tc_pcc = sb("tc_pcc", [128, 4])
        tc_pcc_bd = sb("tc_pcc_bd", [128, 2, 16, 2])
        tc_prob_t = sb("tc_prob_t", [128, 256])
        tc_pv = x_main[:, 0:IMAGES // 2 * D // TOK, :].rearrange("p j (a d) -> p (j a) d", d=D)
        tc_attn_t = sb("tc_attn_t", [128, IMAGES])

        acc = ps("acc", [128, 512])
        scores = ps("scores", [128, 2, 512])
        B0 = ps("B0", [128, 512])
        B1 = ps("B1", [128, 512])
        O = ps("O", [128, 512])
        C0 = ps("C0", [128, 512])
        C1 = ps("C1", [128, 512])

        w_first, w_rest = ev("w_first", 0), ev("w_rest", 0)
        x_in = [ev(f"x_in{i}", 16) for i in range(len(PIECES) + 1)]
        x_used = ev("x_used", len(PIECES))
        stored = ev("stored", 32)
        acc_full, hT_done = ev("acc_full"), ev("hT_done")
        nat_full, nat_done = ev("nat_full"), ev("nat_done")
        bn1_done, mv1_step = ev("bn1_done", TILES), ev("mv1_step", 6)
        var1_done, rstd1_done = ev("var1_done"), ev("rstd1_done")
        hn_done, hnt_full, hnt_done = ev("hn_done", TILES), ev("hnt_full"), ev("hnt_done")
        k_full, kt_done, kbd_done = ev("k_full"), ev("kt_done"), ev("kbd_done", HP)
        q_full, qraw_done, ks_full = ev("q_full"), ev("qraw_done"), ev("ks_full")
        ks_step, cscore_done, qn_done = ev("ks_step", 2), ev("cscore_done"), ev("qn_done")
        qt_full, q_done = ev("qt_full"), ev("q_done", 2)
        v_full, v_done = ev("v_full"), ev("v_done", 2)
        s_full, max_done, sub_done = ev("s_full", TILES), ev("max_done", TILES), ev("sub_done", TILES)
        exp_done, psum_done = ev("exp_done", 2 * TILES), ev("psum_done", TILES)
        sum_done, rec_done = ev("sum_done", 2), ev("rec_done", 2)
        pt_full, pt_done, pv_full = ev("pt_full", TILES), ev("pt_done", TILES), ev("pv_full", TILES)
        pcls_done, acls_done = ev("pcls_done", 2), ev("acls_done", 4)
        o1_done, attn_done = ev("o1_done", 4), ev("attn_done", 8)
        ot_full, ot_done, y_full = ev("ot_full"), ev("ot_done"), ev("y_full")
        hbo_done, h2_done = ev("hbo_done"), ev("h2_done")
        bn2_done, mv2_step = ev("bn2_done", TILES), ev("mv2_step", 6)
        var2_done, rstd2_done = ev("var2_done"), ev("rstd2_done")
        z_done, zt_full, zt_done = ev("z_done", TILES), ev("zt_full"), ev("zt_done", 2)
        zlo_done = ev("zlo_done")
        hhi_done, hlo_done = ev("hhi_done", HC), ev("hlo_done", HC)
        whi_done, wlo_done = ev("whi_done", 0), ev("wlo_done", 0)
        g_full, shift_done, rexp_done = ev("g_full"), ev("shift_done"), ev("rexp_done")
        route_step, comb_done, count_done = ev("route_step", 17), ev("comb_done"), ev("count_done")
        cnt_full, cnt_done = ev("cnt_full"), ev("cnt_done")
        ina_full, inb_full = ev("ina_full", 4), ev("inb_full", 4)
        silu_done, hid_done = ev("silu_done", 4), ev("hid_done", 4)
        sh_full, ysh_done = ev("sh_full"), ev("ysh_done")
        e_full, prod_done = ev("e_full", 2 * TILES), ev("prod_done", 2 * TILES)
        tree1_done, tree2_done, tree_done = ev("tree1_done", TILES), ev("tree2_done", TILES), ev("tree_done", TILES)
        yout_done = ev("yout_done")
        pool_init = ev("pool_init", 0)
        hcls_step, cpow_step = ev("hcls_step", 0), ev("cpow_step", 0)
        cpe, cact, cdve = ev("cpe", 0), ev("cact", 0), ev("cdve", 0)
        tpe, tact, tdve, tpool = ev("tpe", 0), ev("tact", 0), ev("tdve", 0), ev("tpool", 0)

        POOL_INIT = 4
        first_loads = [(w_patch[:, :, :], A["w_patch"]), (w_patch_tail[:, :], A["w_patch_tail"]),
                       (tok_b[:, :], A["tok_b"]), (pos_t[:, :], A["pos_t"]), (const[:, :], A["const"])]
        rest_loads = [(wq[:, :], A["wq"]), (wk[:, :], A["wk"]), (wv[:, :], A["wv"]), (wo[:, :], A["wo"]),
                      (bk_col[:, :], A["bk_col"]), (bv_col[:, :], A["bv_col"]),
                      (bq_row[:, :], A["bq_row"].to_broadcast([128, D])),
                      (bk_row[:, :], A["bk_row"].to_broadcast([128, D])),
                      (bo_row[:, :], A["bo_row"].to_broadcast([128, D])),
                      (cls_row[:, :], A["cls_row"].to_broadcast([128, D])),
                      (pos0_row[:, :], A["pos0_row"].to_broadcast([128, D])),
                      (ln_scale[:, :], A["ln_scale"]), (ln_bias[:, :], A["ln_bias"]),
                      (w_in_raw[0][:, :], A["w_in"][:, 0]), (w_in_raw[1][:, :], A["w_in"][:, 1]),
                       (w_gate[:, 0:2], A["w_gate_g"]), (w_gate[:, 2:NGATE], A["w_gate_e"]),
                      (gate_b[:, 0:2], A["gate_b_g"].to_broadcast([128, 2])),
                      (gate_b[:, 2:NGATE], A["gate_b_e"].to_broadcast([128, EXPERTS])),
                      (w_sout[:, :, :], A["w_sout"]), 
                      (w_eout_raw[0][:, :, :], A["w_eout"][:, 0].rearrange("p (a e) d -> p a (e d)", e=EG)),
                      (w_eout_raw[1][:, :, :], A["w_eout"][:, 1].rearrange("p (a e) d -> p a (e d)", e=EG)),
                      (out_bias[0:EXPERTS, :], A["expert_bias"]), (out_bias[EXPERTS:EXPERTS + 1, :], A["shared_bias"])]
        FIRST, REST = 16 * len(first_loads), 16 * len(rest_loads)

        def groups(engine, body):
            body(0, 0)
            body(1, 1)
            with engine.Fori(2, GROUPS - 3, 2) as g:
                body(g, 0)
                body(g + 1, 1)
            body(GROUPS - 2, 0)
            body(GROUPS - 1, 1)

        def has_next(g):
            return not (isinstance(g, int) and g == GROUPS - 1)

        def has_last(g):
            return not (isinstance(g, int) and g == 0)

        def out_rows(g, b2):
            rows = out.rearrange("(g t b) n d -> g b n t d", t=TILES, b=2)
            return rows[bass.ds(g, 1), b2, 1:SEQ, :, :].rearrange("g n t d -> (g n) t d")

        def prob_bank(p):
            return (B0, B1, B0, B0)[p]

        def ffn_banks(k):
            return (C0, C1) if k % 2 == 0 else (scores[:, 0, :], scores[:, 1, :])

        block = ctx.enter_context(nc.Block())

        @block.sync
        def _(sp):
            def load_x(g):
                for i, (a, b) in enumerate(PIECES):
                    need(sp, x_used, g - 1, i + 1)
                    src = A["x_main"][bass.ds(g, 1), :, a:b, :].rearrange("g p j t -> (g p) j t")
                    sp.dma_start(x_main[:, a:b, :], src).then_inc(x_in[i].sem, 16)
                need(sp, acc_full, g - 1)
                src = A["x_tail"][bass.ds(g, 1), :, :].rearrange("g p t -> (g p) t")
                sp.dma_start(x_tail[:, :], src).then_inc(x_in[-1].sem, 16)

            def store(g):
                need(sp, yout_done, g)
                for b2 in range(2):
                    sp.dma_start(out_rows(g, b2), y_out[64 * b2:64 * b2 + 64, :].rearrange("n (t d) -> n t d", d=D))\
                        .then_inc(stored.sem, 16)

            for dst, src in first_loads[:1]:
                sp.dma_start(dst, src).then_inc(w_first.sem, 16)
            load_x(0)
            for dst, src in rest_loads[14:]:
                sp.dma_start(dst, src).then_inc(w_rest.sem, 16)

            def body(g, par):
                if has_next(g):
                    load_x(g + 1)
                if has_last(g):
                    store(g - 1)

            groups(sp, body)
            store(GROUPS - 1)
            need(sp, yout_done, GROUPS)
            sp.dma_start(out[:, 0, :], y_out[0:IMAGES, 0:D]).then_inc(stored.sem, 16)
            sp.wait_ge(stored.sem, 32 * GROUPS + 16)

        @block.tensor
        def _(pe):
            mm = nc.tensor.matmul

            def transposes(dst, tiles, rows=128):
                for t, src in enumerate(tiles):
                    last = nc.tensor.transpose(dst[0:rows, t * 128:(t + 1) * 128], src, ident)
                return last

            def patch(g, j0, j1):
                if j0 == 0:
                    need(pe, hT_done, g - 1)
                for j in range(j0, j1):
                    for i, (a, _) in enumerate(PIECES):
                        if j == a:
                            need(pe, x_in[i], g)
                    if j < NMAIN:
                        last = mm(acc[:, :], w_patch[:, j, :], x_main[:, j, :], start=(j == 0), stop=False)
                        if any(j == b - 1 for _, b in PIECES):
                            last.then_inc(x_used.sem, 1)
                    else:
                        need(pe, x_in[-1], g)
                        mm(acc[:, :], w_patch_tail[:, :], x_tail[:, :], start=False, stop=True)\
                            .then_inc(acc_full.sem, 1)

            def to_natural(g):
                need(pe, hT_done, g)
                need(pe, h2_done, g - 1)
                transposes(B0, [h_t[:, t * 128:(t + 1) * 128] for t in range(TILES)]).then_inc(nat_full.sem, 1)

            def normed_t(g):
                need(pe, hn_done, g)
                need(pe, zt_done, g - 1)
                transposes(B1, [hn_nat[:, t * 128:(t + 1) * 128] for t in range(TILES)]).then_inc(hnt_full.sem, 1)

            def k_proj(g):
                need(pe, hnt_done, g)
                mm(B1[:, :], wk[:, :], hn_t[:, :], start=True, stop=True).then_inc(k_full.sem, 1)

            def q_proj(g):
                for t in range(TILES):
                    last = mm(B0[:, t * D:(t + 1) * D], hn_t[:, t * 128:(t + 1) * 128], wq[:, :], start=True, stop=True)
                last.then_inc(q_full.sem, 1)

            def k_sums(g):
                need(pe, kt_done, g)
                need(pe, o1_done, g - 1)
                for t in range(TILES):
                    last = mm(O[:, t * 16:(t + 1) * 16], k_t[:, t * 128:(t + 1) * 128], k_sel[:, :], start=True, stop=True)
                last.then_inc(ks_full.sem, 1)

            def v_proj(g):
                need(pe, qraw_done, g)
                for t in range(TILES):
                    last = mm(B0[:, t * D:(t + 1) * D], hn_t[:, t * 128:(t + 1) * 128], wv[:, :], start=True, stop=True)
                last.then_inc(v_full.sem, 1)

            def q_transpose(g):
                need(pe, qn_done, g)
                need(pe, kbd_done, g)
                transposes(B1, [q_nat[:, t * 128:(t + 1) * 128] for t in range(TILES)]).then_inc(qt_full.sem, 1)

            def score(g, p):
                if p == 0:
                    need(pe, q_done, g)
                    if has_last(g):
                        need(pe, hid_done, g - 1)
                else:
                    need(pe, sub_done, g, p)
                for b2 in range(2):
                    b = 2 * p + b2
                    last = mm(scores[:, b2, 0:HP * SEQ], q_mask[:, b, :, :].rearrange("p e n -> p (e n)"),
                              k_bd[:, b, :, :].rearrange("p h m -> p (h m)"), start=True, stop=True)
                last.then_inc(s_full.sem, 1)

            def prob_transpose(g, p):
                need(pe, exp_done, g, 2 * p + 2)
                dst = prob_bank(p)
                if p == 0:
                    need(pe, v_done, g)
                elif p == 1:
                    need(pe, q_done, g)
                else:
                    need(pe, pt_done, g, (1, 3)[p - 2])
                transposes(dst, [probs[p % 2][:, hp, :] for hp in range(HP)]).then_inc(pt_full.sem, 1)

            def prob_v(g, p):
                need(pe, pt_done, g, p + 1)
                if p == 0:
                    need(pe, v_done, g)
                    need(pe, cscore_done, g)
                elif p == 2:
                    need(pe, o1_done, g, 2)
                for hp in range(HP):
                    c = (p % 2) * 256 + hp * 64
                    pair = v_bd[:, bass.ds(g * TILES + p, 1), hp, :, :].rearrange("p a b c -> p (a b c)")
                    last = mm(O[:, c:c + 64], probs_t[p % 2][:, hp * 128:(hp + 1) * 128], pair, start=True, stop=True)
                last.then_inc(pv_full.sem, 1)

            def attn_transpose(g):
                need(pe, attn_done, g)
                need(pe, pt_done, g, 2)
                if has_last(g):
                    need(pe, cnt_done, g - 1)
                transposes(B1, [attn_nat[:, t].rearrange("p h e d -> p (h e d)") for t in range(TILES)])\
                    .then_inc(ot_full.sem, 1)

            def out_proj(g):
                need(pe, ot_done, g)
                need(pe, pt_done, g)
                for t in range(TILES):
                    last = mm(B0[:, t * D:(t + 1) * D], attn_t[:, t * 128:(t + 1) * 128], wo[:, :],
                              start=True, stop=True)
                last.then_inc(y_full.sem, 1)

            def z_transpose(g):
                need(pe, z_done, g)
                transposes(B1, [z_nat[:, t * 128:(t + 1) * 128] for t in range(TILES)]).then_inc(zt_full.sem, 1)

            def gates(g, tiles, rows):
                need(pe, zt_done, g)
                need(pe, prod_done, g - 1)
                for t in range(tiles):
                    last = mm(C0[0:rows, t * NGATE:(t + 1) * NGATE], z_t[:, t * 128:t * 128 + rows], w_gate[:, :],
                              start=True, stop=True)
                last.then_inc(g_full.sem, 1)

            def ffn_in(g, k, n):
                net, c = k // 2, k % 2
                a_bank, b_bank = ffn_banks(k)
                if k == 0:
                    need(pe, route_step, g, 2)
                    need(pe, prod_done, g - 1)
                elif k == 1 and isinstance(g, int) and g == GROUPS:
                    need(pe, hid_done, g - 1)
                elif k == 1:
                    need(pe, sub_done, g)
                else:
                    need(pe, hid_done, g, k - 1)
                need(pe, zlo_done, g)
                for bank, first, full in ((a_bank, c * 128, ina_full), (b_bank, H + c * 128, inb_full)):
                    cols = slice(first, first + 128)
                    mm(bank[:, 0:n], w_in_hi[:, net, cols], z_hi[:, 0:n], start=True, stop=False)
                    mm(bank[:, 0:n], w_in_hi[:, net, cols], z_lo[:, 0:n], start=False, stop=False)
                    mm(bank[:, 0:n], w_in_lo[:, net, cols], z_hi[:, 0:n], start=False, stop=True)\
                        .then_inc(full.sem, 1)

            def counts(g, tiles, rows):
                need(pe, count_done, g)
                if isinstance(g, int) and g >= GROUPS - 1:
                    need(pe, zt_done, g)
                else:
                    need(pe, pt_done, g + 1, 2)
                for t in range(tiles):
                    last = nc.tensor.transpose(B1[0:EXPERTS + 1, t * 128:t * 128 + rows], count[0:rows, t, :],
                                               ident[0:rows, 0:rows])
                last.then_inc(cnt_full.sem, 1)

            def shared_out(g, t, rows, final):
                if t == 0:
                    need(pe, hid_done, g)
                    need(pe, cnt_done, g)
                cols = slice(t * 128, t * 128 + rows)
                dst = C0[0:rows, t * D:(t + 1) * D]
                for c in range(HC):
                    mm(dst, hidden[:, c, cols], w_sout[:, c, :], start=(c == 0), stop=False)
                last = mm(dst, count_t[:, cols], out_bias[:, :], start=False, stop=True)
                if final:
                    last.then_inc(sh_full.sem, 1)

            def expert(g, u, rows):
                t, half = u // 2, u % 2
                if u == 1:
                    need(pe, ysh_done, g)
                elif u >= 2:
                    need(pe, prod_done, g, u - 1)
                if u == 0:
                    need(pe, hlo_done, g)
                dst = (C1, C0)[half]
                cols = slice(t * 128, t * 128 + rows)
                for c in range(HC):
                    w_hi, w_lo = (w[:, c, half * EG:(half + 1) * EG, :].rearrange("p e d -> p (e d)")
                                  for w in (w_eout_hi, w_eout_lo))
                    h_hi, h_lo = hidden_hi[:, c, cols], hidden_lo[:, c, cols]
                    mm(dst[0:rows, :], h_hi, w_hi, start=(c == 0), stop=False)
                    mm(dst[0:rows, :], h_hi, w_lo, start=False, stop=False)
                    last = mm(dst[0:rows, :], h_lo, w_hi, start=False, stop=(c == HC - 1))
                last.then_inc(e_full.sem, 1)

            pe.wait_ge(w_first.sem, FIRST)
            patch(0, 0, NMAIN + 1)
            pe.wait_ge(w_rest.sem, REST)
            pe.wait_ge(hcls_step.sem, 4)
            nc.tensor.transpose(B1[:, 0:128], hn_cls[:, :], ident).then_inc(cpe.sem, 1)
            pe.wait_ge(cact.sem, 1)
            mm(O[:, 0:128], hn_cls_t[:, :], wq[:, :], start=True, stop=True)
            mm(O[:, 128:256], hn_cls_t[:, :], wk[:, :], start=True, stop=True)
            mm(O[:, 256:384], hn_cls_t[:, :], wv[:, :], start=True, stop=True)
            mm(O[:, 384:512], bv_col[:, 0:1].to_broadcast([128, 128]), wo[:, :], start=True, stop=True)\
                .then_inc(cpe.sem, 1)
            to_natural(0)
            pe.wait_ge(cdve.sem, 9)
            nc.tensor.transpose(C0[:, 0:128], k_cls[:, :], ident)
            nc.tensor.transpose(C0[:, 128:256], qn_cls[:, :], ident).then_inc(cpe.sem, 1)
            normed_t(0)

            def body(g, par):
                nxt, last = has_next(g), has_last(g)

                def fill(j0, j1):
                    if nxt:
                        patch(g + 1, j0, j1)

                k_proj(g)
                q_proj(g)
                if last:
                    gates(g - 1, TILES, 128)
                k_sums(g)
                v_proj(g)
                if last:
                    if isinstance(g, int) and g == 1:
                        pe.wait_ge(wlo_done.sem, 4)
                    ffn_in(g - 1, 0, TOK)
                    ffn_in(g - 1, 1, TOK)
                q_transpose(g)
                if last:
                    ffn_in(g - 1, 2, TOK)
                    ffn_in(g - 1, 3, TOK)
                fill(0, 1)
                score(g, 0)
                fill(1, 3)
                score(g, 1)
                fill(3, 4)
                prob_transpose(g, 0)
                fill(4, 5)
                prob_v(g, 0)
                score(g, 2)
                fill(5, 7)
                prob_transpose(g, 1)
                fill(7, 8)
                prob_v(g, 1)
                score(g, 3)
                fill(8, 10)
                prob_transpose(g, 2)
                if last:
                    counts(g - 1, TILES, 128)
                fill(10, 11)
                prob_v(g, 2)
                fill(11, 12)
                prob_transpose(g, 3)
                if last:
                    shared_out(g - 1, 0, 128, False)
                    shared_out(g - 1, 1, 128, False)
                prob_v(g, 3)
                if last:
                    shared_out(g - 1, 2, 128, False)
                    shared_out(g - 1, 3, 128, True)
                    expert(g - 1, 0, 128)
                    expert(g - 1, 1, 128)
                fill(12, 14)
                attn_transpose(g)
                if last:
                    expert(g - 1, 2, 128)
                out_proj(g)
                fill(14, NMAIN + 1)
                if last:
                    expert(g - 1, 3, 128)
                if nxt:
                    to_natural(g + 1)
                if last:
                    expert(g - 1, 4, 128)
                z_transpose(g)
                if last:
                    expert(g - 1, 5, 128)
                    expert(g - 1, 6, 128)
                if nxt:
                    normed_t(g + 1)
                if last:
                    expert(g - 1, 7, 128)

            pe.wait_ge(cdve.sem, 19)
            groups(pe, body)

            L = GROUPS - 1
            gates(L, TILES, 128)
            need(pe, cscore_done, L)
            for half in range(2):
                last = nc.tensor.transpose(O[:, half * 128:(half + 1) * 128],
                                           cls_scores[:, half * 128:(half + 1) * 128], ident)
            last.then_inc(tpe.sem, 1)
            ffn_in(L, 0, TOK)
            ffn_in(L, 1, TOK)
            ffn_in(L, 2, TOK)
            ffn_in(L, 3, TOK)
            pe.wait_ge(tdve.sem, 11)
            for half in range(2):
                last = nc.tensor.transpose(B0[:, half * 128:(half + 1) * 128],
                                           tc_prob[:, 2 * half:2 * half + 2, :].rearrange("p b m -> p (b m)"), ident)
            last.then_inc(tpe.sem, 1)
            counts(L, TILES, 128)
            for t in range(TILES):
                shared_out(L, t, 128, t == TILES - 1)
            for u in range(6):
                expert(L, u, 128)
            pe.wait_ge(tdve.sem, 14)
            pe.wait_ge(tpool.sem, 1)
            mm(O[:, 0:IMAGES], v_cls_rows[:, :], tc_pcc_bd[:, :, :, :].rearrange("p a b c -> p (a b c)"),
               start=True, stop=False, skip_group_check=True)
            for pair in range(IMAGES // 2):
                last = mm(O[:, 2 * pair:2 * pair + 2], tc_pv[:, pair, :], const[:, C_B2:C_B2 + 2],
                          start=False, stop=(pair == IMAGES // 2 - 1), skip_group_check=True)
            last.then_inc(tpe.sem, 1)
            expert(L, 6, 128)
            pe.wait_ge(tact.sem, 4)
            mm(B0[0:IMAGES, 0:D], tc_attn_t[:, :], wo[:, :], start=True, stop=True).then_inc(tpe.sem, 1)
            expert(L, 7, 128)
            need(pe, z_done, GROUPS, 1)
            nc.tensor.transpose(B1[:, 0:IMAGES], z_nat[0:IMAGES, 0:128], ident[0:IMAGES, 0:IMAGES])\
                .then_inc(zt_full.sem, 1)
            gates(GROUPS, 1, IMAGES)
            for k in range(4):
                ffn_in(GROUPS, k, IMAGES)
            counts(GROUPS, 1, IMAGES)
            shared_out(GROUPS, 0, IMAGES, True)
            expert(GROUPS, 0, IMAGES)
            expert(GROUPS, 1, IMAGES)

        @block.scalar
        def _(act):
            def go(dst, src, func=ACT.Copy, **kw):
                return nc.scalar.activation(dst, src, func, **kw)

            def natural(g, par):
                need(act, nat_full, g)
                need(act, h2_done, g - 2)
                go(h_nat[par][:, :], B0[:, :]).then_inc(nat_done.sem, 1)

            def normed_t(g):
                need(act, hnt_full, g)
                go(hn_t[:, :], B1[:, :]).then_inc(hnt_done.sem, 1)

            def k_plain(g):
                need(act, k_full, g)
                go(k_t[:, :], B1[:, :], ACT.Relu, bias=bk_col[:, 0:1]).then_inc(kt_done.sem, 1)

            def q_masked(g):
                need(act, qt_full, g)
                for e in range(2):
                    go(q_mask[:, :, e, :], B1[:, :].rearrange("p (b n) -> p b n", n=NPATCH),
                       scale=const[:, C_PAR + e:C_PAR + e + 1]).then_inc(q_done.sem, 1)

            def v_blocks(g):
                need(act, v_full, g)
                for b2 in range(2):
                    r = slice(64 * b2, 64 * b2 + 64)
                    go(v_bd[r, bass.ds(g * TILES, TILES), :, b2, :], B0[r, :].rearrange("p (a h c) -> p a h c", h=HP, c=32))\
                        .then_inc(v_done.sem, 1)

            def k_blocks(g):
                need(act, k_full, g)
                for hp in range(HP):
                    r = slice(32 * hp, 32 * hp + 32)
                    go(k_bd[r, :, hp, 0:NPATCH], B1[r, :].rearrange("p (b m) -> p b m", m=NPATCH), ACT.Relu,
                       bias=bk_col[r, 0:1])\
                        .then_inc(kbd_done.sem, 1)

            def exps(g, p):
                need(act, sub_done, g, p + 1)
                need(act, pt_full, *((g, p - 1) if p >= 2 else (g - 1, p + 3)))
                need(act, psum_done, *((g, p - 1) if p >= 2 else (g - 1, p + 3)))
                need(act, pcls_done, g - 1, p // 2 + 1)
                go(probs[p % 2][:, :, :].rearrange("p h (b m) -> p h b m", b=2),
                   shift[p % 2][:, :, :, 0:NPATCH].rearrange("p b h m -> p h b m"), ACT.Exp).then_inc(exp_done.sem, 1)
                go(exp_cls[:, p], shift[p % 2][:, :, :, NPATCH].rearrange("p b h -> p h b"), ACT.Exp)\
                    .then_inc(exp_done.sem, 1)

            def probs_out(g, p):
                need(act, pt_full, g, p + 1)
                if p >= 2:
                    need(act, pv_full, g, p - 1)
                go(probs_t[p % 2][:, :], prob_bank(p)[:, :]).then_inc(pt_done.sem, 1)

            def attn_out(g):
                need(act, ot_full, g)
                go(attn_t[:, :], B1[:, :]).then_inc(ot_done.sem, 1)

            def z_out(g, n):
                need(act, zt_full, g)
                need(act, inb_full, g - 1)
                for dst in (z_hi, z_t):
                    go(dst[:, 0:n], B1[:, 0:n], ACT.Identity, scale=ln_scale[:, 0:1], bias=ln_bias[:, 0:1])\
                        .then_inc(zt_done.sem, 1)

            def hidden_high(g, c, n):
                need(act, hid_done, g, HC + c + 1)
                go(hidden_hi[:, c, 0:n], silu[c][:, 0:n]).then_inc(hhi_done.sem, 1)

            def route_exp(g, tiles, rows):
                need(act, shift_done, g)
                go(e_exp[0:rows, 0:2 * tiles, :], e_shift[0:rows, 0:2 * tiles, :], ACT.Exp).then_inc(rexp_done.sem, 1)

            def silus(g, k, n):
                need(act, ina_full, g, k + 1)
                if k >= 2:
                    need(act, hid_done, g, k - 1)
                else:
                    need(act, hlo_done, g - 1, k + 1)
                go(silu[k % 2][:, 0:n], ffn_banks(k)[0][:, 0:n], ACT.Silu).then_inc(silu_done.sem, 1)

            def counts_out(g, n):
                need(act, cnt_full, g)
                go(count_t[:, 0:n], B1[0:EXPERTS + 1, 0:n]).then_inc(cnt_done.sem, 1)

            for dst, src in first_loads[1:]:
                act.dma_start(dst, src).then_inc(w_first.sem, 16)
            for dst, src in rest_loads[:14]:
                act.dma_start(dst, src).then_inc(w_rest.sem, 16)
            act.wait_ge(cpe.sem, 1)
            go(hn_cls_t[:, :], B1[:, 0:128]).then_inc(cact.sem, 1)
            natural(0, 0)
            act.wait_ge(cpe.sem, 3)
            go(k_cls_t[:, :], C0[:, 0:1]).then_inc(cact.sem, 1)
            go(qn_cls_t[:, :], C0[:, 128:129]).then_inc(cact.sem, 1)
            act.wait_ge(pool_init.sem, POOL_INIT)
            act.wait_ge(cact.sem, 3)
            for hp in range(HP):
                r = slice(32 * hp, 32 * hp + 32)
                go(k_bd[r, :, hp, NPATCH:SEQ], k_cls_t[r, 0:1].unsqueeze(2).to_broadcast([32, GROUP_IMAGES, 1]))\
                    .then_inc(cact.sem, 1)
            normed_t(0)

            def body(g, par):
                nxt, last = has_next(g), has_last(g)
                k_plain(g)
                k_blocks(g)
                v_blocks(g)
                if last:
                    silus(g - 1, 0, TOK)
                    silus(g - 1, 1, TOK)
                q_masked(g)
                if last:
                    silus(g - 1, 2, TOK)
                    silus(g - 1, 3, TOK)
                exps(g, 0)
                if last:
                    hidden_high(g - 1, 0, TOK)
                exps(g, 1)
                if last:
                    route_exp(g - 1, TILES, 128)
                    hidden_high(g - 1, 1, TOK)
                else:
                    act.wait_ge(w_rest.sem, REST)
                    for i in range(2):
                        go(w_in_hi[:, i], w_in_raw[i][:, :]).then_inc(whi_done.sem, 1)
                    for c in range(HC):
                        go(w_eout_hi[:, c].rearrange("p e d -> p (e d)"), w_eout_raw[c].rearrange("p a b -> p (a b)"))\
                            .then_inc(whi_done.sem, 1)
                probs_out(g, 0)
                exps(g, 2)
                probs_out(g, 1)
                exps(g, 3)
                probs_out(g, 2)
                if last:
                    counts_out(g - 1, TOK)
                probs_out(g, 3)
                attn_out(g)
                if nxt:
                    natural(g + 1, 1 - par)
                z_out(g, TOK)
                if nxt:
                    normed_t(g + 1)

            groups(act, body)
            L = GROUPS - 1
            route_exp(L, TILES, 128)
            act.wait_ge(tdve.sem, 4)
            go(tc_exp[:, :, :], tc_shift[:, :, :], ACT.Exp).then_inc(tact.sem, 1)
            go(tc_cc_exp[:, :], tc_cc[:, :], ACT.Exp).then_inc(tact.sem, 1)
            for k in range(4):
                silus(L, k, TOK)
            act.wait_ge(tpe.sem, 2)
            go(tc_prob_t[:, :], B0[:, 0:256]).then_inc(tact.sem, 1)
            hidden_high(L, 0, TOK)
            hidden_high(L, 1, TOK)
            counts_out(L, TOK)
            act.wait_ge(tpe.sem, 3)
            go(tc_attn_t[:, :], O[:, 0:IMAGES]).then_inc(tact.sem, 1)
            z_out(GROUPS, IMAGES)
            route_exp(GROUPS, 1, IMAGES)
            for k in range(4):
                silus(GROUPS, k, IMAGES)
            hidden_high(GROUPS, 0, IMAGES)
            hidden_high(GROUPS, 1, IMAGES)
            counts_out(GROUPS, IMAGES)

        @block.vector
        def _(dve):
            v = nc.vector

            def bcast(ap, n):
                return ap.unsqueeze(len(ap.shape)).to_broadcast(list(ap.shape) + [n])

            def moments(src, stats, m, var, scale, offset, bn_done, step, var_done, g, tiles, rows):
                r, T = slice(0, rows), slice(0, tiles)
                for t in range(tiles):
                    v.bn_stats(stats[r, t, :], src[r, t * 128:(t + 1) * 128]).then_inc(bn_done.sem, 1)
                need(dve, bn_done, g, tiles)
                v.tensor_tensor(m[r, 1, T], stats[r, T, 1], stats[r, T, 4], ALU.add).then_inc(step.sem, 1)
                v.tensor_tensor(m[r, 2, T], stats[r, T, 1], stats[r, T, 4], ALU.subtract).then_inc(step.sem, 1)
                v.tensor_tensor(m[r, 3, T], stats[r, T, 2], stats[r, T, 5], ALU.add).then_inc(step.sem, 1)
                need(dve, step, g, 2)
                v.tensor_scalar(m[r, 0, T], m[r, 1, T], 0.5, None, ALU.mult).then_inc(step.sem, 1)
                v.scalar_tensor_tensor(m[r, 4, T], m[r, 2, T], D / 4.0, m[r, 2, T], ALU.mult, ALU.mult)\
                    .then_inc(step.sem, 1)
                need(dve, step, g, 5)
                v.tensor_tensor(m[r, 5, T], m[r, 3, T], m[r, 4, T], ALU.add).then_inc(step.sem, 1)
                need(dve, step, g, 6)
                v.tensor_scalar(var[r, T], m[r, 5, T], scale / D, offset, ALU.mult, ALU.add).then_inc(var_done.sem, 1)

            def normalise(dst, src, mv, rstd, done, tiles, rows):
                for t in range(tiles):
                    v.tensor_scalar(dst[0:rows, t * 128:(t + 1) * 128], src[0:rows, t * 128:(t + 1) * 128],
                                    mv[0:rows, 0, t:t + 1], rstd[0:rows, t:t + 1], ALU.subtract, ALU.mult)\
                        .then_inc(done.sem, 1)

            def tokens(g):
                need(dve, acc_full, g)
                v.scalar_tensor_tensor(h_t[:, :].rearrange("p (b n) -> p b n", n=NPATCH),
                                       acc[:, :].rearrange("p (b n) -> p b n", n=NPATCH), tok_b[:, 0:1],
                                       pos_t[:, :].unsqueeze(1).to_broadcast([128, GROUP_IMAGES, NPATCH]),
                                       ALU.add, ALU.mult).then_inc(hT_done.sem, 1)

            def norm1(g, par):
                need(dve, nat_done, g)
                moments(h_nat[par], stats1, mv1, var1, 1.0, LN_EPS, bn1_done, mv1_step, var1_done, g, TILES, 128)
                need(dve, rstd1_done, g)
                normalise(hn_nat, h_nat[par], mv1, rstd1, hn_done, TILES, 128)

            def q_add(g):
                need(dve, q_full, g)
                need(dve, qt_full, g - 1)
                v.tensor_tensor(q_nat[:, :].rearrange("p (t d) -> p t d", d=D),
                                B0[:, :].rearrange("p (t d) -> p t d", d=D),
                                bq_row[:, :].unsqueeze(1).to_broadcast([128, TILES, D]), ALU.add)\
                    .then_inc(qraw_done.sem, 1)

            def q_norm(g):
                need(dve, ks_full, g)
                sums = O[:, 0:TILES * 16].rearrange("p (t n) -> p t n", n=16)
                v.tensor_scalar(q_sum_eps[:, :, :], sums[:, :, 0:HEADS], ATTN_EPS, None, ALU.add).then_inc(ks_step.sem, 1)
                v.tensor_copy(cls_scores[:, bass.ds(g * (TILES * HEADS), TILES * HEADS)]
                              .rearrange("p (t n) -> p t n", n=HEADS), sums[:, :, HEADS:16]).then_inc(cscore_done.sem, 1)
                need(dve, ks_step, g, 1)
                v.reciprocal(q_rec[:, :, :], q_sum_eps[:, :, :]).then_inc(ks_step.sem, 1)
                need(dve, ks_step, g, 2)
                need(dve, qraw_done, g)
                v.scalar_tensor_tensor(q_nat[:, :].rearrange("p (h d) -> p h d", d=DH),
                                       q_nat[:, :].rearrange("p (h d) -> p h d", d=DH), 0.0,
                                       bcast(q_rec[:, :, :].rearrange("p t h -> p (t h)"), DH), ALU.max, ALU.mult)\
                    .then_inc(qn_done.sem, 1)

            def row_maxes(g, p):
                need(dve, s_full, g, p + 1)
                s = scores[:, :, 0:HP * SEQ].rearrange("p b (h m) -> p b h m", m=SEQ)
                v.tensor_reduce(row_max[p % 2][:, :, :], s, AX.X, ALU.max).then_inc(max_done.sem, 1)
                need(dve, max_done, g, p + 1)
                need(dve, exp_done, *((g, 2 * (p - 1)) if p >= 2 else (g - 1, 2 * (p + 3))))
                v.tensor_tensor(shift[p % 2][:, :, :, :], s, bcast(row_max[p % 2][:, :, :], SEQ), ALU.subtract)\
                    .then_inc(sub_done.sem, 1)

            def row_sums(g, p):
                need(dve, exp_done, g, 2 * p + 2)
                v.tensor_reduce(patch_sum[:, p], probs[p % 2][:, :, :].rearrange("p h (b m) -> p h b m", b=2), AX.X,
                                ALU.add).then_inc(psum_done.sem, 1)
                if p % 2:
                    half = p // 2
                    pair = slice(2 * half, 2 * half + 2)
                    need(dve, psum_done, g, p + 1)
                    v.tensor_tensor(row_sum[:, pair], patch_sum[:, pair], exp_cls[:, pair], ALU.add)\
                        .then_inc(sum_done.sem, 1)
                    need(dve, sum_done, g, half + 1)
                    need(dve, pcls_done, g - 1, half + 1)
                    v.reciprocal(row_rec[:, pair], row_sum[:, pair])\
                        .then_inc(rec_done.sem, 1)

            def attn_scale(g, half):
                need(dve, pv_full, g, 2 * half + 2)
                need(dve, rec_done, g, half + 1)
                o = O[:, :].rearrange("p (a b e d) -> p a b e d", a=8, b=2, e=2)
                for e in range(2):
                    r = slice(64 * e, 64 * e + 64)
                    rec = row_rec[r, 2 * half:2 * half + 2].rearrange("p a h b -> p (a h) b")
                    v.tensor_tensor(attn_patch[half][r], o[r, :, :, e, :], bcast(rec, DH), ALU.mult)\
                        .then_inc(o1_done.sem, 1)

            def attn_sum(g, half):
                need(dve, acls_done, g, 2 * half + 2)
                need(dve, o1_done, g, 2 * half + 2)
                if half == 0:
                    need(dve, ot_full, g - 1)
                cls = attn_cls[half][:, :, :, :, :].rearrange("p a h b d -> p (a h) b d")
                dst = attn_nat[:, 2 * half:2 * half + 2].rearrange("p a h e d -> p (a h) e d")
                for b2 in range(2):
                    for e in range(2):
                        o, r = slice(64 * b2, 64 * b2 + 64), slice(64 * e, 64 * e + 64)
                        v.tensor_tensor(dst[o, :, e, :], attn_patch[half][r, :, b2, :], cls[r, :, b2, :], ALU.add)\
                            .then_inc(attn_done.sem, 1)

            def residual(g, par):
                need(dve, y_full, g)
                need(dve, hbo_done, g)
                v.tensor_tensor(h2[par][:, :], B0[:, :], h_nat[par][:, :], ALU.add).then_inc(h2_done.sem, 1)

            def norm2(g, src, tiles, rows):
                need(dve, h2_done, g)
                moments(src, stats2, mv2, var2, 1.0 + LN_EPS, LN_EPS * LN_EPS, bn2_done, mv2_step, var2_done, g, tiles,
                        rows)
                need(dve, rstd2_done, g)
                normalise(z_nat, src, mv2, rstd2, z_done, tiles, rows)

            def logits(g, tiles, rows):
                r, T, S = slice(0, rows), tiles, 2 * tiles
                gates_ps = C0[r, 0:T * NGATE].rearrange("p (t n) -> p t n", n=NGATE)
                gb = gate_b[r, :].unsqueeze(1).to_broadcast([rows, T, NGATE])
                need(dve, g_full, g)
                v.tensor_tensor(g_logit[r, 0:T], gates_ps[:, :, 0:2], gb[:, :, 0:2], ALU.add).then_inc(route_step.sem, 1)
                v.tensor_tensor(e_logit[r, 0:S].rearrange("p (t a) e -> p t (a e)", a=2), gates_ps[:, :, 2:NGATE],
                                gb[:, :, 2:NGATE], ALU.add).then_inc(route_step.sem, 1)

            def choose(g, tiles, rows):
                def chained(ins):
                    nonlocal n
                    ins.then_inc(route_step.sem, 1)
                    n += 1
                    need(dve, route_step, g, n)

                n = 2
                r, T, S = slice(0, rows), tiles, 2 * tiles
                need(dve, route_step, g, n)
                chained(v.tensor_tensor(g_sel[r, 0:T, 1], g_logit[r, 0:T, 1], g_logit[r, 0:T, 0], ALU.is_gt))
                chained(v.tensor_scalar(g_sel[r, 0:T, 0], g_sel[r, 0:T, 1], -1.0, 1.0, ALU.mult, ALU.add))
                chained(v.tensor_reduce(e_max[r, 0:S], e_logit[r, 0:S], AX.X, ALU.max))
                need(dve, rexp_done, g - 1)
                v.tensor_tensor(e_shift[r, 0:S], e_logit[r, 0:S], bcast(e_max[r, 0:S], EG), ALU.subtract)\
                    .then_inc(shift_done.sem, 1)
                lj = e_logit[r, 0:S].unsqueeze(2).to_broadcast([rows, S, EG, EG])
                ge = e_ge[r, 0:S].rearrange("p s (i j) -> p s i j", j=EG)
                chained(v.tensor_tensor(ge, lj, bcast(e_logit[r, 0:S], EG), ALU.is_ge))
                chained(v.tensor_tensor(e_ge[r, 0:S], e_ge[r, 0:S],
                                        const[r, C_TRI:C_TRI + 16].unsqueeze(1).to_broadcast([rows, S, 16]), ALU.mult))
                chained(v.tensor_reduce(e_row[r, 0:S], ge, AX.X, ALU.add))
                chained(v.tensor_reduce(e_col[r, 0:S], ge.rearrange("p s i j -> p s j i"), AX.X, ALU.add))
                chained(v.tensor_tensor(e_top[r, 0:S], e_row[r, 0:S], e_col[r, 0:S], ALU.subtract))
                chained(v.tensor_tensor(e_row[r, 0:S], e_top[r, 0:S],
                                        const[r, C_THR:C_THR + EG].unsqueeze(1).to_broadcast([rows, S, EG]), ALU.is_lt))
                cnt = count[r, 0:T, 0:EXPERTS].rearrange("p t (a e) -> p t a e", e=EG)
                need(dve, cnt_full, g - 1)
                v.tensor_tensor(cnt, e_row[r, 0:S].rearrange("p (t a) e -> p t a e", a=2), bcast(g_sel[r, 0:T], EG),
                                ALU.mult).then_inc(count_done.sem, 1)

            def weights(g, tiles, rows):
                def chained(ins):
                    nonlocal n
                    ins.then_inc(route_step.sem, 1)
                    n += 1
                    need(dve, route_step, g, n)

                n = 11
                r, T, S = slice(0, rows), tiles, 2 * tiles
                need(dve, count_done, g)
                need(dve, rexp_done, g)
                ex = e_exp[r, 0:S].rearrange("p (t a) e -> p t (a e)", a=2)
                chained(v.tensor_tensor(e_keep[r, 0:T], ex, count[r, 0:T, 0:EXPERTS], ALU.mult))
                chained(v.tensor_tensor(e_group[r, 0:T].rearrange("p t (a e) -> p t a e", e=EG),
                                        e_exp[r, 0:S].rearrange("p (t a) e -> p t a e", a=2), bcast(g_sel[r, 0:T], EG),
                                        ALU.mult))
                chained(v.tensor_reduce(e_den[r, 0, 0:T], e_keep[r, 0:T], AX.X, ALU.add))
                chained(v.tensor_reduce(e_den[r, 1, 0:T], e_group[r, 0:T], AX.X, ALU.add))
                chained(v.scalar_tensor_tensor(e_den[r, 2, 0:T], e_den[r, 1, 0:T], 1e-8, e_den[r, 0, 0:T],
                                               ALU.mult, ALU.add))
                chained(v.reciprocal(e_den[r, 3, 0:T], e_den[r, 2, 0:T]))
                v.tensor_tensor(comb[r, 0:T], e_keep[r, 0:T], bcast(e_den[r, 3, 0:T], EXPERTS), ALU.mult)\
                    .then_inc(comb_done.sem, 1)
                assert n == route_step.per, n

            def hidden_mul(g, k, n):
                net, c = k // 2, k % 2
                need(dve, silu_done, g, k + 1)
                need(dve, inb_full, g, k + 1)
                dst = silu[c] if net else hidden[:, c]
                v.tensor_tensor(dst[:, 0:n], silu[k % 2][:, 0:n], ffn_banks(k)[1][:, 0:n], ALU.mult)\
                    .then_inc(hid_done.sem, 1)

            def shared_add(g, src, tiles, rows):
                need(dve, sh_full, g)
                need(dve, stored, g - 1)
                v.tensor_tensor(y_out[0:rows, 0:tiles * D], C0[0:rows, 0:tiles * D], src[0:rows, 0:tiles * D], ALU.add)\
                    .then_inc(ysh_done.sem, 1)

            def weigh(g, u, rows):
                t, half = u // 2, u % 2
                need(dve, e_full, g, u + 1)
                if u == 0:
                    need(dve, comb_done, g)
                if half == 0:
                    if t >= 2:
                        need(dve, tree_done, g, t - 1)
                    else:
                        need(dve, tree_done, g - 1, t + 3)
                src = (C1, C0)[half]
                v.tensor_tensor(prod[t % 2][0:rows, half, :].rearrange("p (e d) -> p e d", d=D),
                                src[0:rows, :].rearrange("p (e d) -> p e d", d=D),
                                bcast(comb[0:rows, t, half * EG:(half + 1) * EG], D), ALU.mult).then_inc(prod_done.sem, 1)

            def output(g, tiles, rows):
                need(dve, ysh_done, g)
                need(dve, tree_done, g, tiles)
                v.tensor_tensor(y_out[0:rows, 0:tiles * D], y_out[0:rows, 0:tiles * D],
                                routed[0:rows, 0:tiles].rearrange("p t d -> p (t d)"), ALU.add).then_inc(yout_done.sem, 1)

            dve.wait_ge(w_first.sem, FIRST)
            dve.wait_ge(w_rest.sem, REST)
            v.tensor_tensor(h_cls[:, :], cls_row[:, :], pos0_row[:, :], ALU.mult).then_inc(hcls_step.sem, 1)
            v.tensor_copy(k_sel[:, 0:HEADS], const[:, C_HEAD:C_HEAD + HEADS]).then_inc(cdve.sem, 1)
            dve.wait_ge(hcls_step.sem, 1)
            v.bn_stats(cls_stats[:, :], h_cls[:, :]).then_inc(hcls_step.sem, 1)
            dve.wait_ge(hcls_step.sem, 2)
            v.bn_aggr(cls_mv[:, :], cls_stats[:, :]).then_inc(hcls_step.sem, 1)
            dve.wait_ge(cpow_step.sem, 2)
            dve.wait_ge(hcls_step.sem, 3)
            v.tensor_scalar(hn_cls[:, :], h_cls[:, :], cls_mv[:, 0:1], cls_rstd[:, 0:1], ALU.subtract, ALU.mult)\
                .then_inc(hcls_step.sem, 1)
            tokens(0)
            dve.wait_ge(cpe.sem, 2)
            v.tensor_tensor(q_cls_raw[:, :], O[:, 0:128], bq_row[:, :], ALU.add).then_inc(cdve.sem, 1)
            v.tensor_tensor(k_cls_raw[:, :], O[:, 128:256], bk_row[:, :], ALU.add).then_inc(cdve.sem, 1)
            dve.wait_ge(cdve.sem, 3)
            v.tensor_scalar(q_cls[:, :], q_cls_raw[:, :], 0.0, None, ALU.max).then_inc(cdve.sem, 1)
            v.tensor_scalar(k_cls[:, :], k_cls_raw[:, :], 0.0, None, ALU.max).then_inc(cdve.sem, 1)
            dve.wait_ge(cdve.sem, 5)
            kv = k_cls[:, :].rearrange("p (h d) -> p h d", d=DH)
            v.tensor_reduce(k_cls_sum[:, 0:8], kv, AX.X, ALU.add).then_inc(cdve.sem, 1)
            dve.wait_ge(cdve.sem, 6)
            v.tensor_scalar(k_cls_sum[:, 8:16], k_cls_sum[:, 0:8], ATTN_EPS, None, ALU.add).then_inc(cdve.sem, 1)
            dve.wait_ge(cdve.sem, 7)
            v.reciprocal(k_cls_sum[:, 16:24], k_cls_sum[:, 8:16]).then_inc(cdve.sem, 1)
            dve.wait_ge(cdve.sem, 8)
            v.tensor_tensor(qn_cls[:, :].rearrange("p (h d) -> p h d", d=DH),
                            q_cls[:, :].rearrange("p (h d) -> p h d", d=DH), bcast(k_cls_sum[:, 16:24], DH),
                            ALU.mult).then_inc(cdve.sem, 1)
            v.tensor_copy(v_cls[:, :], O[:, 256:384]).then_inc(cdve.sem, 1)
            v.tensor_tensor(bo2[:, :], O[:, 384:512], bo_row[:, :], ALU.add).then_inc(cdve.sem, 1)
            dve.wait_ge(cdve.sem, 11)
            for e in range(2):
                r = slice(64 * e, 64 * e + 64)
                v.tensor_copy(v_cls_hp[r], v_cls[r].rearrange("p (h e d) -> p h e d", e=2, d=DH)[:, :, e, :])\
                    .then_inc(cdve.sem, 1)
            v.tensor_tensor(cc_mul[:, :], qn_cls[:, :], k_cls[:, :], ALU.mult).then_inc(cdve.sem, 1)
            v.tensor_tensor(v_cls_rows[:, :], v_cls[:, :], const[:, C_HMASK:C_HMASK + 128], ALU.mult)\
                .then_inc(cdve.sem, 1)
            v.tensor_tensor(h_cls_bo[:, :], h_cls[:, :], bo2[:, :], ALU.add).then_inc(cdve.sem, 1)
            dve.wait_ge(cdve.sem, 16)
            v.tensor_reduce(cc_row[:, :], cc_mul[:, :].rearrange("p (h d) -> p h d", d=DH), AX.X, ALU.add)\
                .then_inc(cdve.sem, 1)
            dve.wait_ge(cdve.sem, 17)
            v.tensor_tensor(cc_pick[:, :], cc_row[:, :], const[:, C_HROW:C_HROW + 8], ALU.mult).then_inc(cdve.sem, 1)
            dve.wait_ge(cdve.sem, 18)
            dve.wait_ge(cact.sem, 3)
            v.tensor_scalar(k_sel[:, HEADS:16], const[:, C_HEAD:C_HEAD + HEADS], qn_cls_t[:, 0:1], None, ALU.mult)\
                .then_inc(cdve.sem, 1)
            v.tensor_reduce(cc_col[:, :], cc_pick[:, :], AX.X, ALU.add).then_inc(cdve.sem, 1)
            norm1(0, 0)

            def body(g, par):
                nxt, last = has_next(g), has_last(g)
                q_add(g)
                if last:
                    logits(g - 1, TILES, 128)
                q_norm(g)
                if last:
                    hidden_mul(g - 1, 0, TOK)
                    hidden_mul(g - 1, 1, TOK)
                    hidden_mul(g - 1, 2, TOK)
                    hidden_mul(g - 1, 3, TOK)
                row_maxes(g, 0)
                row_maxes(g, 1)
                row_sums(g, 0)
                if last:
                    choose(g - 1, TILES, 128)
                row_maxes(g, 2)
                row_sums(g, 1)
                attn_scale(g, 0)
                row_maxes(g, 3)
                if last:
                    weights(g - 1, TILES, 128)
                row_sums(g, 2)
                attn_sum(g, 0)
                row_sums(g, 3)
                attn_scale(g, 1)
                attn_sum(g, 1)
                if last:
                    shared_add(g - 1, h2[1 - par], TILES, 128)
                    weigh(g - 1, 0, 128)
                    weigh(g - 1, 1, 128)
                    weigh(g - 1, 2, 128)
                residual(g, par)
                norm2(g, h2[par], TILES, 128)
                if nxt:
                    tokens(g + 1)
                if last:
                    weigh(g - 1, 3, 128)
                    weigh(g - 1, 4, 128)
                if nxt:
                    norm1(g + 1, 1 - par)
                if last:
                    weigh(g - 1, 5, 128)
                    weigh(g - 1, 6, 128)
                    weigh(g - 1, 7, 128)
                    output(g - 1, TILES, 128)

            groups(dve, body)

            L = GROUPS - 1
            logits(L, TILES, 128)
            choose(L, TILES, 128)
            weights(L, TILES, 128)
            dve.wait_ge(tpe.sem, 1)
            s = O[:, 0:256].rearrange("p (a m) -> p a m", m=NPATCH)
            v.tensor_reduce(tc_max0[:, :], s, AX.X, ALU.max).then_inc(tdve.sem, 1)
            dve.wait_ge(tdve.sem, 1)
            v.tensor_scalar(tc_max[:, :], tc_max0[:, :], cc_col[:, 0:1], None, ALU.max).then_inc(tdve.sem, 1)
            dve.wait_ge(tdve.sem, 2)
            v.tensor_tensor(tc_shift[:, :, :], s, bcast(tc_max[:, :], NPATCH), ALU.subtract).then_inc(tdve.sem, 1)
            v.tensor_scalar(tc_cc[:, :], tc_max[:, :], -1.0, cc_col[:, 0:1], ALU.mult, ALU.add).then_inc(tdve.sem, 1)
            hidden_mul(L, 0, TOK)
            dve.wait_ge(tact.sem, 2)
            v.tensor_reduce(tc_sum[:, 0, :], tc_exp[:, :, :], AX.X, ALU.add).then_inc(tdve.sem, 1)
            dve.wait_ge(tdve.sem, 5)
            v.tensor_tensor(tc_sum[:, 1, :], tc_sum[:, 0, :], tc_cc_exp[:, :], ALU.add).then_inc(tdve.sem, 1)
            dve.wait_ge(tdve.sem, 6)
            v.reciprocal(tc_sum[:, 2, :], tc_sum[:, 1, :]).then_inc(tdve.sem, 1)
            dve.wait_ge(tdve.sem, 7)
            v.tensor_tensor(tc_pcc[:, :], tc_cc_exp[:, :], tc_sum[:, 2, :], ALU.mult).then_inc(tdve.sem, 1)
            dve.wait_ge(tdve.sem, 8)
            for half in range(2):
                v.tensor_tensor(tc_pcc_bd[:, half],
                                tc_pcc[:, 2 * half:2 * half + 2].unsqueeze(1).to_broadcast([128, 16, 2]),
                                bcast(const[:, C_PMASK:C_PMASK + 16], 2), ALU.mult).then_inc(tdve.sem, 1)
            v.tensor_tensor(tc_prob[:, :, :], tc_exp[:, :, :], bcast(tc_sum[:, 2, :], NPATCH), ALU.mult)\
                .then_inc(tdve.sem, 1)
            hidden_mul(L, 1, TOK)
            hidden_mul(L, 2, TOK)
            hidden_mul(L, 3, TOK)
            dve.wait_ge(tact.sem, 3)
            v.tensor_tensor(tc_pv[0:64, :, :].rearrange("p a (h d) -> p (a h) d", d=DH)[:, 0:128].rearrange("p (a e) d -> p a e d", e=2),
                            v_bd[0:64, 0:16, :, 0, :].rearrange("p a h (e d) -> p (a h) e d", e=2),
                            bcast(tc_prob_t[0:64, 0:128].rearrange("p (a e) -> p a e", e=2), DH), ALU.mult)\
                .then_inc(tdve.sem, 1)
            shared_add(L, h2[1], TILES, 128)
            weigh(L, 0, 128)
            weigh(L, 1, 128)
            v.tensor_tensor(tc_pv[0:64, :, :].rearrange("p a (h d) -> p (a h) d", d=DH)[:, 128:256].rearrange("p (a e) d -> p a e d", e=2),
                            v_bd[0:64, 16:32, :, 0, :].rearrange("p a h (e d) -> p (a h) e d", e=2),
                            bcast(tc_prob_t[0:64, 128:256].rearrange("p (a e) -> p a e", e=2), DH), ALU.mult)\
                .then_inc(tdve.sem, 1)
            v.tensor_copy(tc_sum[:, 0, :], tc_sum[:, 2, :]).then_inc(tdve.sem, 1)
            for u in range(2, 7):
                weigh(L, u, 128)
            dve.wait_ge(tpe.sem, 4)
            v.tensor_tensor(h2[0][0:IMAGES, 0:D], B0[0:IMAGES, 0:D], h_cls_bo[0:IMAGES, :], ALU.add)\
                .then_inc(h2_done.sem, 1)
            norm2(GROUPS, h2[0], 1, IMAGES)
            weigh(L, 7, 128)
            output(L, TILES, 128)
            logits(GROUPS, 1, IMAGES)
            choose(GROUPS, 1, IMAGES)
            weights(GROUPS, 1, IMAGES)
            for k in range(4):
                hidden_mul(GROUPS, k, IMAGES)
            shared_add(GROUPS, h2[0], 1, IMAGES)
            weigh(GROUPS, 0, IMAGES)
            weigh(GROUPS, 1, IMAGES)
            output(GROUPS, 1, IMAGES)

        @block.gpsimd
        def _(pool):
            q = nc.gpsimd

            def norm_scale1(g):
                need(pool, var1_done, g)
                q.tensor_tensor(rstd1[:, :], var1[:, :], neg_half[:, :], ALU.pow).then_inc(rstd1_done.sem, 1)

            def norm_scale2(g, tiles, rows):
                need(pool, var2_done, g)
                q.tensor_tensor(rstd2[0:rows, 0:tiles], var2[0:rows, 0:tiles], neg_half[0:rows, 0:tiles], ALU.pow)\
                    .then_inc(rstd2_done.sem, 1)

            def bias_residual(g, par):
                need(pool, nat_done, g)
                need(pool, hn_done, g)
                q.tensor_tensor(h_nat[par][:, :].rearrange("p (t d) -> p t d", d=D),
                                h_nat[par][:, :].rearrange("p (t d) -> p t d", d=D),
                                bo2[:, :].unsqueeze(1).to_broadcast([128, TILES, D]), ALU.add).then_inc(hbo_done.sem, 1)

            def class_value(g, half):
                need(pool, rec_done, g, half + 1)
                need(pool, attn_done, g - 1, 4 * half + 4)
                pair = slice(2 * half, 2 * half + 2)
                q.tensor_tensor(p_cls[half][:, :, :, :], exp_cls[:, pair],
                                row_rec[:, pair], ALU.mult).then_inc(pcls_done.sem, 1)
                need(pool, pcls_done, g, half + 1)
                for a in range(2):
                    q.tensor_tensor(attn_cls[half][:, a],
                                    p_cls[half][:, a].unsqueeze(3).to_broadcast([128, HP, 2, DH]),
                                    v_cls_hp[:, :, :].unsqueeze(2).to_broadcast([128, HP, 2, DH]), ALU.mult)\
                        .then_inc(acls_done.sem, 1)

            def z_low(g, n):
                need(pool, zt_done, g)
                need(pool, inb_full, g - 1)
                q.tensor_tensor(z_lo[:, 0:n], z_t[:, 0:n], z_hi[:, 0:n].bitcast(F32), ALU.subtract)\
                    .then_inc(zlo_done.sem, 1)

            def hidden_low(g, c, n):
                need(pool, hhi_done, g, c + 1)
                q.tensor_tensor(hidden_lo[:, c, 0:n], silu[c][:, 0:n],
                                hidden_hi[:, c, 0:n].bitcast(F32), ALU.subtract).then_inc(hlo_done.sem, 1)

            def expert_sum(g, t, rows):
                need(pool, prod_done, g, 2 * t + 2)
                r, p = slice(0, rows), prod[t % 2]
                q.tensor_tensor(p[r, 0, :], p[r, 0, :], p[r, 1, :], ALU.add).then_inc(tree1_done.sem, 1)
                need(pool, tree1_done, g, t + 1)
                q.tensor_tensor(p[r, 0, 0:2 * D], p[r, 0, 0:2 * D], p[r, 0, 2 * D:4 * D], ALU.add)\
                    .then_inc(tree2_done.sem, 1)
                need(pool, tree2_done, g, t + 1)
                if t == 0:
                    need(pool, yout_done, g - 1)
                q.tensor_tensor(routed[r, t, :], p[r, 0, 0:D], p[r, 0, D:2 * D], ALU.add)\
                    .then_inc(tree_done.sem, 1)

            q.memset(neg_half[:, :], -0.5).then_inc(pool_init.sem, 1)
            q.memset(k_bd[:, :, :, :], 0.0).then_inc(pool_init.sem, 1)
            q.memset(v_bd[:, :, :, :, :], 0.0).then_inc(pool_init.sem, 1)
            q.memset(count[:, :, :], 1.0).then_inc(pool_init.sem, 1)
            pool.wait_ge(pool_init.sem, POOL_INIT)
            pool.wait_ge(hcls_step.sem, 3)
            q.tensor_scalar(cls_var[:, :], cls_mv[:, 1:2], LN_EPS, None, ALU.add).then_inc(cpow_step.sem, 1)
            pool.wait_ge(cpow_step.sem, 1)
            q.tensor_tensor(cls_rstd[:, :], cls_var[:, :], neg_half[:, 0:1], ALU.pow).then_inc(cpow_step.sem, 1)
            norm_scale1(0)
            pool.wait_ge(cdve.sem, 16)

            def body(g, par):
                nxt, last = has_next(g), has_last(g)
                if last:
                    z_low(g - 1, TOK)
                bias_residual(g, par)
                if last:
                    hidden_low(g - 1, 0, TOK)
                    hidden_low(g - 1, 1, TOK)
                else:
                    for i in range(2):
                        pool.wait_ge(whi_done.sem, i + 1)
                        q.tensor_tensor(w_in_lo[:, i], w_in_raw[i][:, :], w_in_hi[:, i].bitcast(F32), ALU.subtract)\
                            .then_inc(wlo_done.sem, 1)
                    for c in range(HC):
                        pool.wait_ge(whi_done.sem, 3 + c)
                        q.tensor_tensor(w_eout_lo[:, c].rearrange("p e d -> p (e d)"),
                                        w_eout_raw[c].rearrange("p a b -> p (a b)"),
                                        w_eout_hi[:, c].rearrange("p e d -> p (e d)").bitcast(F32), ALU.subtract)\
                            .then_inc(wlo_done.sem, 1)
                class_value(g, 0)
                class_value(g, 1)
                if last:
                    expert_sum(g - 1, 0, 128)
                norm_scale2(g, TILES, 128)
                if last:
                    expert_sum(g - 1, 1, 128)
                if nxt:
                    norm_scale1(g + 1)
                if last:
                    expert_sum(g - 1, 2, 128)
                    expert_sum(g - 1, 3, 128)

            groups(pool, body)
            L = GROUPS - 1
            z_low(L, TOK)
            pool.wait_ge(tact.sem, 3)
            q.tensor_tensor(tc_pv[64:128, :, :].rearrange("p a (h e d) -> p (a h) e d", e=2, d=DH),
                            v_bd[64:128, :, :, 1, :].rearrange("p a h (e d) -> p (a h) e d", e=2),
                            tc_prob_t[64:128, :].rearrange("p (a e) -> p a e", e=2).unsqueeze(3)
                            .to_broadcast([64, 128, 2, DH]), ALU.mult).then_inc(tpool.sem, 1)
            pool.wait_ge(tpool.sem, 1)
            hidden_low(L, 0, TOK)
            hidden_low(L, 1, TOK)
            expert_sum(L, 0, 128)
            expert_sum(L, 1, 128)
            expert_sum(L, 2, 128)
            norm_scale2(GROUPS, 1, IMAGES)
            expert_sum(L, 3, 128)
            z_low(GROUPS, IMAGES)
            hidden_low(GROUPS, 0, IMAGES)
            hidden_low(GROUPS, 1, IMAGES)
            expert_sum(GROUPS, 0, IMAGES)


OUT_SHAPE = (IMAGES, SEQ, D)


def kernel(x, L0_tok_W, L0_tok_b, L0_tok_class_token, L0_tok_pos_embed, L0_attn_Wq, L0_attn_bq, L0_attn_Wk,
           L0_attn_bk, L0_attn_Wv, L0_attn_bv, L0_attn_Wo, L0_attn_bo, L0_ffn_ln_scale, L0_ffn_ln_bias,
           L0_ffn_shared_in_w, L0_ffn_shared_out_w, L0_ffn_shared_out_b, L0_ffn_expert_in_w,
           L0_ffn_expert_out_weight, L0_ffn_expert_out_bias, L0_ffn_group_gate_w, L0_ffn_expert_gate_w,
           L0_ffn_group_bias, L0_ffn_expert_bias):
    import concourse.bacc as bacc
    from concourse.bass_utils import run_bass_kernel_spmd

    xg = np.asarray(x).reshape(GROUPS, GROUP_IMAGES, CHANNELS, GRID, PATCH, GRID, PATCH)
    xg = xg.transpose(0, 2, 4, 6, 1, 3, 5).reshape(GROUPS, IN_D, TOK)
    wp = np.asarray(L0_tok_W).T
    main = NMAIN * 128
    pos = np.asarray(L0_tok_pos_embed)

    def t(a):
        return np.asarray(a).T

    def col(a):
        return np.asarray(a).reshape(-1, 1)

    def row(a):
        return np.asarray(a).reshape(1, -1)

    layouts = {
        "x_main": xg[:, :main].reshape(GROUPS, NMAIN, 128, TOK).transpose(0, 2, 1, 3),
        "x_tail": xg[:, main:],
        "w_patch": wp[:main].reshape(NMAIN, 128, D).transpose(1, 0, 2),
        "w_patch_tail": wp[main:],
        "tok_b": col(L0_tok_b), "pos_t": pos[1:].T, "pos0_row": pos[0:1], "cls_row": L0_tok_class_token,
        "wq": t(L0_attn_Wq), "wk": t(L0_attn_Wk), "wv": t(L0_attn_Wv), "wo": t(L0_attn_Wo),
        "bk_col": col(L0_attn_bk), "bv_col": col(L0_attn_bv),
        "bq_row": row(L0_attn_bq), "bk_row": row(L0_attn_bk), "bo_row": row(L0_attn_bo),
        "ln_scale": col(L0_ffn_ln_scale), "ln_bias": col(L0_ffn_ln_bias),
        "w_in": np.stack([t(L0_ffn_shared_in_w), t(L0_ffn_expert_in_w)], 1),
        "w_gate_g": t(L0_ffn_group_gate_w), "w_gate_e": t(L0_ffn_expert_gate_w),
        "gate_b_g": row(L0_ffn_group_bias), "gate_b_e": row(L0_ffn_expert_bias),
        "w_sout": t(L0_ffn_shared_out_w).reshape(HC, 128, D).transpose(1, 0, 2),
        "w_eout": np.asarray(L0_ffn_expert_out_weight).transpose(2, 0, 1).reshape(HC, 128, EXPERTS, D)
                    .transpose(1, 0, 2, 3),
        "expert_bias": L0_ffn_expert_out_bias, "shared_bias": row(L0_ffn_shared_out_b),
        "const": shape_constants(),
    }
    nc = bacc.Bacc("TRN2", target_bir_lowering=False, num_devices=1)
    arrays, A = {}, {}
    for name, a in layouts.items():
        a = np.ascontiguousarray(a)
        arrays[f"in_{name}"] = a
        A[name] = nc.dram_tensor(f"in_{name}", a.shape, mybir.dt.from_np(a.dtype), kind="ExternalInput").ap()
    out = nc.dram_tensor("out_tokens", OUT_SHAPE, F32, kind="ExternalOutput").ap()
    vit_tower(nc, A, out)
    r = run_bass_kernel_spmd(nc, [arrays], core_ids=[0])
    return r.results[0]["out_tokens"]
```

```python
from contextlib import ExitStack

import numpy as np
import concourse.bass as bass
from concourse import mybir

F32 = mybir.dt.float32
F32R = mybir.dt.float32r
ALU = mybir.AluOpType
ACT = mybir.ActivationFunctionType
AX = mybir.AxisListType

IMAGES, CHANNELS, SIDE, GRID = 64, 3, 224, 8
PATCH = SIDE // GRID
NPATCH = GRID * GRID
SEQ = NPATCH + 1
D = 128
IN_D = CHANNELS * PATCH * PATCH
NMAIN = IN_D // 128
NTAIL = IN_D - NMAIN * 128
GROUP_IMAGES = 8
GROUPS = IMAGES // GROUP_IMAGES
TOK = GROUP_IMAGES * NPATCH
TILES = TOK // 128
HEADS, DH = 8, 16
HP = HEADS // 2
H = 256
HC = H // 128
EXPERTS, EG = 8, 4
NGATE = 2 + EXPERTS
ATTN_EPS = 1e-6
LN_EPS = 1e-5
AHEAD = 6
PIECES = [(j, j + 3) for j in range(0, NMAIN, 3)]

C_ID, C_PAR, C_TRI, C_THR, C_HROW, C_HMASK, C_PMASK = 0, 128, 130, 146, 150, 158, 286
C_B2, C_HEAD = 302, 304
NCONST = 312
V_POS, V_TOK_B, V_BK, V_BV, V_SCALE, V_BIAS = NCONST, NCONST + 64, NCONST + 65, NCONST + 66, NCONST + 67, NCONST + 68
NCOLS = NCONST + 69


def shape_constants():
    c = np.zeros((128, NCONST), np.float32)
    p = np.arange(128)
    c[:, C_ID:C_ID + 128] = np.eye(128)
    c[:, C_PAR:C_PAR + 2] = (p[:, None] // DH % 2) == np.arange(2)
    i, j = np.meshgrid(np.arange(EG), np.arange(EG), indexing="ij")
    c[:, C_TRI:C_TRI + 16] = (j < i).reshape(1, 16)
    c[:, C_THR:C_THR + EG] = np.arange(EG)[None] - 1
    c[:, C_HROW:C_HROW + 8] = (p[:, None] % 8) == np.arange(8)
    c[:, C_HMASK:C_HMASK + 128] = (p[:, None] % 8) == (np.arange(128)[None] // DH)
    c[:, C_PMASK:C_PMASK + 16] = (p[:, None] // 8) == np.arange(16)
    c[:, C_B2:C_B2 + 2] = (p[:, None] // 64) == np.arange(2)
    c[:, C_HEAD:C_HEAD + HEADS] = (p[:, None] // DH) == np.arange(HEADS)
    return c


class Event:

    def __init__(self, ctx, nc, name, per=1):
        self.sem = ctx.enter_context(nc.semaphore(name))
        self.per = per


def need(engine, event, g, k=None):
    value = event.per * g + (event.per if k is None else k)
    if isinstance(value, int) and value <= 0:
        return
    engine.wait_ge(event.sem, value)


def vit_tower(nc, A, out):
    ctx = ExitStack()
    with ctx:
        def sb(name, shape, dt=F32):
            return ctx.enter_context(nc.sbuf_tensor(name, shape, dt))

        def ps(name, shape):
            return ctx.enter_context(nc.psum_tensor(name, shape, F32))

        def ev(name, per=1):
            return Event(ctx, nc, name, per)

        const = sb("const", [128, NCOLS])
        w_patch = sb("w_patch", [128, NMAIN, D])
        w_patch_tail = sb("w_patch_tail", [NTAIL, D])
        bq_row = sb("bq_row", [128, D])
        w_in_lo = sb("w_in_lo", [128, 2, 2 * H], F32R)
        w_in_hi = sb("w_in_hi", [128, 2, 2 * H], F32R)
        w_gate = sb("w_gate", [128, NGATE])
        gate_b = sb("gate_b", [128, NGATE])
        w_sout = sb("w_sout", [128, HC, D])
        w_eout_lo = sb("w_eout_lo", [128, HC, EXPERTS, D], F32R)
        w_eout_hi = sb("w_eout_hi", [128, HC, EXPERTS, D], F32R)
        out_bias = sb("out_bias", [EXPERTS + 1, D])

        w_attn = sb("w_attn", [128, 4, D])
        wq, wk, wv, wo = (w_attn[:, i, :] for i in range(4))
        ident = const[:, C_ID:C_ID + 128]
        pos_t = const[:, V_POS:V_POS + NPATCH]
        tok_b, bk_col, bv_col, ln_scale, ln_bias = (const[:, v:v + 1] for v in (V_TOK_B, V_BK, V_BV, V_SCALE, V_BIAS))

        x_main = sb("x_main", [128, NMAIN, TOK])
        x_tail = sb("x_tail", [NTAIL, TOK])
        h_t = sb("h_t", [128, TOK])
        h_nat = [sb(f"h_nat{i}", [128, TOK]) for i in range(2)]
        stats1 = sb("stats1", [128, TILES, 6])
        mv1 = sb("mv1", [128, 6, TILES])
        var1 = sb("var1", [128, TILES])
        rstd1 = sb("rstd1", [128, TILES])
        neg_half = sb("neg_half", [128, TILES])
        hn_nat = sb("hn_nat", [128, TOK])
        hn_t = sb("hn_t", [128, TOK])
        q_mask = sb("q_mask", [128, GROUP_IMAGES, 2, NPATCH])
        k_t = sb("k_t", [128, TOK])
        k_sel = sb("k_sel", [128, 2 * HEADS])
        q_sum_eps = sb("q_sum_eps", [128, TILES, HEADS])
        q_rec = sb("q_rec", [128, TILES, HEADS])
        q_nat = sb("q_nat", [128, TOK])
        k_bd = sb("k_bd", [128, GROUP_IMAGES, HP, SEQ])
        v_bd = sb("v_bd", [128, IMAGES // 2, HP, 2, 32])
        shift = [sb(f"shift{i}", [128, 2, HP, SEQ]) for i in range(2)]
        probs = [sb(f"probs{i}", [128, HP, 2 * NPATCH]) for i in range(2)]
        exp_cls = sb("exp_cls", [128, TILES, HP, 2])
        patch_sum = sb("patch_sum", [128, TILES, HP, 2])
        row_max = [sb(f"row_max{i}", [128, 2, HP]) for i in range(2)]
        row_sum = sb("row_sum", [128, TILES, HP, 2])
        row_rec = sb("row_rec", [128, TILES, HP, 2])
        probs_t = [sb(f"probs_t{i}", [128, 512]) for i in range(2)]
        attn_patch = [sb(f"attn_patch{i}", [128, 8, 2, DH]) for i in range(2)]
        p_cls = [sb(f"p_cls{i}", [128, 2, HP, 2]) for i in range(2)]
        attn_cls = [sb(f"attn_cls{i}", [128, 2, HP, 2, DH]) for i in range(2)]
        attn_nat = sb("attn_nat", [128, TILES, HP, 2, DH])
        attn_t = sb("attn_t", [128, TOK])
        h2 = [sb(f"h2_{i}", [128, TOK]) for i in range(2)]
        stats2 = sb("stats2", [128, TILES, 6])
        mv2 = sb("mv2", [128, 6, TILES])
        var2 = sb("var2", [128, TILES])
        rstd2 = sb("rstd2", [128, TILES])
        z_nat = sb("z_nat", [128, TOK])
        z_t = sb("z_t", [128, TOK])
        z_hi = sb("z_hi", [128, TOK], F32R)
        z_lo = sb("z_lo", [128, TOK], F32R)
        cls_scores = sb("cls_scores", [128, IMAGES // 2 * HEADS])
        g_logit = sb("g_logit", [128, TILES, 2])
        e_logit = sb("e_logit", [128, TILES * 2, EG])
        g_sel = sb("g_sel", [128, TILES, 2])
        e_max = sb("e_max", [128, TILES * 2])
        e_shift = sb("e_shift", [128, TILES * 2, EG])
        e_exp = sb("e_exp", [128, TILES * 2, EG])
        e_ge = sb("e_ge", [128, TILES * 2, EG * EG])
        e_row = sb("e_row", [128, TILES * 2, EG])
        e_col = sb("e_col", [128, TILES * 2, EG])
        e_top = sb("e_top", [128, TILES * 2, EG])
        count = sb("count", [128, TILES, EXPERTS + 1])
        e_keep = sb("e_keep", [128, TILES, EXPERTS])
        e_group = sb("e_group", [128, TILES, EXPERTS])
        e_den = sb("e_den", [128, 4, TILES])
        comb = sb("comb", [128, TILES, EXPERTS])
        count_t = sb("count_t", [EXPERTS + 1, TOK])
        silu = [sb(f"silu{i}", [128, TOK]) for i in range(2)]
        hidden = sb("hidden", [128, HC, TOK])
        hidden_hi = sb("hidden_hi", [128, HC, TOK], F32R)
        hidden_lo = sb("hidden_lo", [128, HC, TOK], F32R)
        prod = [sb(f"prod{i}", [128, 2, EG * D]) for i in range(2)]
        routed = sb("routed", [128, TILES, D])
        y_out = sb("y_out", [128, TOK])
        free = [b[:, i * D:(i + 1) * D] for b in (hidden[:, 0], hidden[:, 1], y_out, routed.rearrange("p t d -> p (t d)"))
                for i in range(4)]
        (bk_row, bo_row, cls_row, pos0_row, h_cls, hn_cls, hn_cls_t, q_cls_raw, q_cls, k_cls_raw, k_cls, qn_cls, v_cls,
         cc_mul) = free[:14]
        w_in_raw, w_eout_raw = silu, prod
        cls_stats = sb("cls_stats", [128, 6])
        cls_mv = sb("cls_mv", [128, 2])
        cls_var = sb("cls_var", [128, 1])
        cls_rstd = sb("cls_rstd", [128, 1])
        k_cls_sum = sb("k_cls_sum", [128, 3 * HEADS])
        k_cls_t = sb("k_cls_t", [128, 1])
        qn_cls_t = sb("qn_cls_t", [128, 1])
        v_cls_hp = sb("v_cls_hp", [128, HP, DH])
        bo2 = sb("bo2", [128, D])
        cc_row = sb("cc_row", [128, HEADS])
        cc_pick = sb("cc_pick", [128, HEADS])
        cc_col = sb("cc_col", [128, 1])
        v_cls_rows = sb("v_cls_rows", [128, D])
        h_cls_bo = sb("h_cls_bo", [128, D])
        tc_max0 = sb("tc_max0", [128, 4])
        tc_max = sb("tc_max", [128, 4])
        tc_shift = x_main[:, 8, 0:4 * NPATCH].rearrange("p (a m) -> p a m", m=NPATCH)
        tc_exp = x_main[:, 9, 0:4 * NPATCH].rearrange("p (a m) -> p a m", m=NPATCH)
        tc_cc = sb("tc_cc", [128, 4])
        tc_cc_exp = sb("tc_cc_exp", [128, 4])
        tc_sum = sb("tc_sum", [128, 3, 4])
        tc_prob = x_main[:, 10, 0:4 * NPATCH].rearrange("p (a m) -> p a m", m=NPATCH)
        tc_pcc = sb("tc_pcc", [128, 4])
        tc_pcc_bd = sb("tc_pcc_bd", [128, 2, 16, 2])
        tc_prob_t = sb("tc_prob_t", [128, 256])
        tc_pv = x_main[:, 0:IMAGES // 2 * D // TOK, :].rearrange("p j (a d) -> p (j a) d", d=D)
        table_row = sb("table_row", [128, 1])
        y_cls, routed_cls = x_main[:, 12, 0:D], x_main[:, 12, D:2 * D].rearrange("p (t d) -> p t d", d=D)
        tc_attn_t = sb("tc_attn_t", [128, IMAGES])

        acc = ps("acc", [128, 512])
        scores = ps("scores", [128, 2, 512])
        B0 = ps("B0", [128, 512])
        B1 = ps("B1", [128, 512])
        O = ps("O", [128, 512])
        C0 = ps("C0", [128, 512])
        C1 = ps("C1", [128, 512])

        w_piece = [ev(f"w_piece{i}", 0) for i in range(len(PIECES))]
        w_first, w_row, w_ffn = ev("w_first", 0), ev("w_row", 0), ev("w_ffn", 0)
        x_in = [ev(f"x_in{i}", 16) for i in range(len(PIECES) + 1)]
        x_used = ev("x_used", len(PIECES))
        stored = ev("stored", 32)
        acc_full, hT_done = ev("acc_full"), ev("hT_done")
        nat_full, nat_done = ev("nat_full"), ev("nat_done")
        bn1_done, mv1_step = ev("bn1_done", TILES), ev("mv1_step", 6)
        var1_done, rstd1_done = ev("var1_done"), ev("rstd1_done")
        hn_done, hnt_full, hnt_done = ev("hn_done", TILES), ev("hnt_full"), ev("hnt_done")
        k_full, kt_done, kbd_done = ev("k_full"), ev("kt_done"), ev("kbd_done", HP)
        q_full, qraw_done, ks_full = ev("q_full"), ev("qraw_done"), ev("ks_full")
        ks_step, cscore_done, qn_done = ev("ks_step", 2), ev("cscore_done"), ev("qn_done")
        qt_full, q_done = ev("qt_full"), ev("q_done", 2)
        v_full, v_done = ev("v_full"), ev("v_done", 2)
        s_full, max_done, sub_done = ev("s_full", TILES), ev("max_done", TILES), ev("sub_done", TILES)
        exp_done, psum_done = ev("exp_done", 2 * TILES), ev("psum_done", TILES)
        sum_done, rec_done = ev("sum_done", 2), ev("rec_done", 2)
        pt_full, pt_done, pv_full = ev("pt_full", TILES), ev("pt_done", TILES), ev("pv_full", TILES)
        pcls_done, acls_done = ev("pcls_done", 2), ev("acls_done", 4)
        o1_done, attn_done = ev("o1_done", 4), ev("attn_done", 8)
        ot_full, ot_done, y_full = ev("ot_full"), ev("ot_done"), ev("y_full")
        hbo_done, h2_done = ev("hbo_done"), ev("h2_done")
        bn2_done, mv2_step = ev("bn2_done", TILES), ev("mv2_step", 6)
        var2_done, rstd2_done = ev("var2_done"), ev("rstd2_done")
        z_done, zt_full, zt_done = ev("z_done", TILES), ev("zt_full"), ev("zt_done", 2)
        zlo_done = ev("zlo_done")
        hhi_done, hlo_done = ev("hhi_done", HC), ev("hlo_done", HC)
        whi_done, wlo_done = ev("whi_done", 0), ev("wlo_done", 0)
        g_full, shift_done, rexp_done = ev("g_full"), ev("shift_done"), ev("rexp_done")
        route_step, comb_done, count_done = ev("route_step", 17), ev("comb_done"), ev("count_done")
        cnt_full, cnt_done = ev("cnt_full"), ev("cnt_done")
        ina_full, inb_full = ev("ina_full", 4), ev("inb_full", 4)
        silu_done, hid_done = ev("silu_done", 4), ev("hid_done", 4)
        sh_full, ysh_done = ev("sh_full"), ev("ysh_done")
        e_full, prod_done = ev("e_full", 2 * TILES), ev("prod_done", 2 * TILES)
        tree1_done, tree2_done, tree_done = ev("tree1_done", TILES), ev("tree2_done", TILES), ev("tree_done", TILES)
        yout_done = ev("yout_done")
        table_done = ev("table_done", 2)
        pool_init = ev("pool_init", 0)
        hcls_step, cpow_step = ev("hcls_step", 0), ev("cpow_step", 0)
        cpe, cact, cdve = ev("cpe", 0), ev("cact", 0), ev("cdve", 0)
        tpe, tact, tdve, tpool = ev("tpe", 0), ev("tact", 0), ev("tdve", 0), ev("tpool", 0)

        POOL_INIT = 4
        first_loads = [(w_patch_tail[:, :], A["w_patch_tail"]), (const[:, :], A["const"])]
        row_loads = [(hidden[:, 0, :], A["rows"].to_broadcast([128, 4 * D])), (w_attn[:, :, :], A["w_attn"]),
                     (bq_row[:, :], A["bq_row"].to_broadcast([128, D]))]
        ffn_loads = [(w_in_raw[0][:, :], A["w_in"][:, 0]), (w_in_raw[1][:, :], A["w_in"][:, 1]),
                     (w_eout_raw[0][:, :, :], A["w_eout"][:, 0].rearrange("p (a e) d -> p a (e d)", e=EG)),
                     (w_eout_raw[1][:, :, :], A["w_eout"][:, 1].rearrange("p (a e) d -> p a (e d)", e=EG)),
                     (w_gate[:, :], A["w_gate"]), (gate_b[:, :], A["gate_b"].to_broadcast([128, NGATE])),
                     (w_sout[:, :, :], A["w_sout"]), (out_bias[:, :], A["out_bias"])]
        FIRST, ROW, FFN = 16 * len(first_loads), 16 * len(row_loads), 16 * len(ffn_loads)

        def groups(engine, body):
            body(0, 0)
            body(1, 1)
            with engine.Fori(2, GROUPS - 3, 2) as g:
                body(g, 0)
                body(g + 1, 1)
            body(GROUPS - 2, 0)
            body(GROUPS - 1, 1)

        def has_next(g):
            return not (isinstance(g, int) and g == GROUPS - 1)

        def has_last(g):
            return not (isinstance(g, int) and g == 0)

        def out_rows(g, b2):
            rows = out.rearrange("(g t b) n d -> g b n t d", t=TILES, b=2)
            return rows[bass.ds(g, 1), b2, 1:SEQ, :, :].rearrange("g n t d -> (g n) t d")

        def prob_bank(p):
            return (B0, B1, B0, B0)[p]

        def is_class(g):
            return isinstance(g, int) and g == GROUPS

        def ffn_banks(g, k):
            if is_class(g):
                bank = (O, acc)[k % 2]
                return bank[:, 0:64], bank[:, 64:128]
            return (C0, C1) if k % 2 == 0 else (scores[:, 0, :], scores[:, 1, :])

        def is_int(g, value):
            return isinstance(g, int) and g == value

        def z_bank(g):
            return C0 if is_int(g, 0) else B1

        def gate_bank(g):
            return B0 if is_class(g) else C1

        def count_bank(g):
            return B0[:, 128:256] if is_class(g) else B1

        def shared_bank(g):
            return B0[:, 256:384] if is_class(g) else C0

        def expert_bank(u):
            return (C1, scores[:, 0, :], scores[:, 1, :], C0)[u % 4]

        block = ctx.enter_context(nc.Block())

        @block.sync
        def _(sp):
            def load_x(g):
                for i, (a, b) in enumerate(PIECES):
                    need(sp, x_used, g - 1, i + 1)
                    src = A["x_main"][bass.ds(g, 1), :, a:b, :].rearrange("g p j t -> (g p) j t")
                    sp.dma_start(x_main[:, a:b, :], src).then_inc(x_in[i].sem, 16)
                need(sp, acc_full, g - 1)
                src = A["x_tail"][bass.ds(g, 1), :, :].rearrange("g p t -> (g p) t")
                sp.dma_start(x_tail[:, :], src).then_inc(x_in[-1].sem, 16)

            def store(g):
                need(sp, yout_done, g)
                for b2 in range(2):
                    sp.dma_start(out_rows(g, b2), y_out[64 * b2:64 * b2 + 64, :].rearrange("n (t d) -> n t d", d=D))\
                        .then_inc(stored.sem, 16)

            load_x(0)
            load_x(1)
            for dst, src in ffn_loads:
                sp.dma_start(dst, src).then_inc(w_ffn.sem, 16)
            load_x(2)
            load_x(3)
            with sp.Fori(4, GROUPS) as g:
                store(g - 4)
                load_x(g)
            for g in range(GROUPS - 4, GROUPS):
                store(g)
            need(sp, yout_done, GROUPS)
            sp.dma_start(out[:, 0, :], y_cls[0:IMAGES, 0:D]).then_inc(stored.sem, 16)
            sp.wait_ge(stored.sem, 32 * GROUPS + 16)

        @block.tensor
        def _(pe):
            mm = nc.tensor.matmul

            def transposes(dst, tiles, rows=128):
                for t, src in enumerate(tiles):
                    last = nc.tensor.transpose(dst[0:rows, t * 128:(t + 1) * 128], src, ident)
                return last

            def patch(g, j0, j1):
                if j0 == 0:
                    need(pe, hT_done, g - 1)
                for j in range(j0, j1):
                    for i, (a, _) in enumerate(PIECES):
                        if j == a:
                            need(pe, x_in[i], g)
                            if isinstance(g, int) and g == 0:
                                pe.wait_ge(w_piece[i].sem, 16)
                    if j < NMAIN:
                        last = mm(acc[:, :], w_patch[:, j, :], x_main[:, j, :], start=(j == 0), stop=False)
                        if any(j == b - 1 for _, b in PIECES):
                            last.then_inc(x_used.sem, 1)
                    else:
                        need(pe, x_in[-1], g)
                        mm(acc[:, :], w_patch_tail[:, :], x_tail[:, :], start=False, stop=True)\
                            .then_inc(acc_full.sem, 1)

            def to_natural(g):
                need(pe, hT_done, g)
                if not (isinstance(g, int) and g <= 1):
                    need(pe, hid_done, g - 2)
                transposes(C1, [h_t[:, t * 128:(t + 1) * 128] for t in range(TILES)]).then_inc(nat_full.sem, 1)

            def normed_t(g):
                need(pe, hn_done, g)
                need(pe, ot_done, g - 1)
                transposes(B1, [hn_nat[:, t * 128:(t + 1) * 128] for t in range(TILES)]).then_inc(hnt_full.sem, 1)

            def k_proj(g):
                need(pe, hnt_done, g)
                if not is_int(g, 1):
                    need(pe, zt_done, g - 1)
                mm(B1[:, :], wk[:, :], hn_t[:, :], start=True, stop=True).then_inc(k_full.sem, 1)

            def q_proj(g):
                need(pe, h2_done, g - 1)
                for t in range(TILES):
                    last = mm(B0[:, t * D:(t + 1) * D], hn_t[:, t * 128:(t + 1) * 128], wq[:, :], start=True, stop=True)
                last.then_inc(q_full.sem, 1)

            def k_sums(g):
                need(pe, kt_done, g)
                need(pe, o1_done, g - 1)
                for t in range(TILES):
                    last = mm(O[:, t * 16:(t + 1) * 16], k_t[:, t * 128:(t + 1) * 128], k_sel[:, :], start=True, stop=True)
                last.then_inc(ks_full.sem, 1)

            def v_proj(g):
                need(pe, qraw_done, g)
                for t in range(TILES):
                    last = mm(B0[:, t * D:(t + 1) * D], hn_t[:, t * 128:(t + 1) * 128], wv[:, :], start=True, stop=True)
                last.then_inc(v_full.sem, 1)

            def q_transpose(g):
                need(pe, qn_done, g)
                need(pe, kbd_done, g)
                transposes(B1, [q_nat[:, t * 128:(t + 1) * 128] for t in range(TILES)]).then_inc(qt_full.sem, 1)

            def score(g, p):
                if p == 0:
                    need(pe, q_done, g)
                    if has_last(g):
                        need(pe, hid_done, g - 1)
                else:
                    need(pe, sub_done, g, p)
                for b2 in range(2):
                    b = 2 * p + b2
                    last = mm(scores[:, b2, 0:HP * SEQ], q_mask[:, b, :, :].rearrange("p e n -> p (e n)"),
                              k_bd[:, b, :, :].rearrange("p h m -> p (h m)"), start=True, stop=True)
                last.then_inc(s_full.sem, 1)

            def prob_transpose(g, p):
                need(pe, exp_done, g, 2 * p + 2)
                dst = prob_bank(p)
                if p == 0:
                    need(pe, v_done, g)
                elif p == 1:
                    need(pe, q_done, g)
                else:
                    need(pe, pt_done, g, (1, 3)[p - 2])
                transposes(dst, [probs[p % 2][:, hp, :] for hp in range(HP)]).then_inc(pt_full.sem, 1)

            def prob_v(g, p):
                need(pe, pt_done, g, p + 1)
                if p == 0:
                    need(pe, v_done, g)
                    need(pe, cscore_done, g)
                elif p == 2:
                    need(pe, o1_done, g, 2)
                for hp in range(HP):
                    c = (p % 2) * 256 + hp * 64
                    pair = v_bd[:, bass.ds(g * TILES + p, 1), hp, :, :].rearrange("p a b c -> p (a b c)")
                    last = mm(O[:, c:c + 64], probs_t[p % 2][:, hp * 128:(hp + 1) * 128], pair, start=True, stop=True)
                last.then_inc(pv_full.sem, 1)

            def attn_transpose(g):
                need(pe, attn_done, g)
                need(pe, pt_done, g, 2)
                if has_last(g):
                    need(pe, cnt_done, g - 1)
                transposes(B1, [attn_nat[:, t].rearrange("p h e d -> p (h e d)") for t in range(TILES)])\
                    .then_inc(ot_full.sem, 1)

            def out_proj(g):
                need(pe, ot_done, g)
                need(pe, pt_done, g)
                for t in range(TILES):
                    last = mm(B0[:, t * D:(t + 1) * D], attn_t[:, t * 128:(t + 1) * 128], wo[:, :],
                              start=True, stop=True)
                last.then_inc(y_full.sem, 1)

            def z_transpose(g):
                need(pe, z_done, g)
                if has_next(g):
                    need(pe, hnt_done, g + 1)
                transposes(z_bank(g), [z_nat[:, t * 128:(t + 1) * 128] for t in range(TILES)]).then_inc(zt_full.sem, 1)

            def gates(g, tiles, rows):
                need(pe, zt_done, g)
                if not is_class(g):
                    need(pe, prod_done, g - 1, 5)
                for t in range(tiles):
                    last = mm(gate_bank(g)[0:rows, t * NGATE:(t + 1) * NGATE], z_t[:, t * 128:t * 128 + rows], w_gate[:, :],
                              start=True, stop=True)
                last.then_inc(g_full.sem, 1)

            def ffn_in(g, k, n):
                net, c = k // 2, k % 2
                a_bank, b_bank = ffn_banks(g, k)
                if is_class(g) and k < 2:
                    pass
                elif k == 0:
                    need(pe, route_step, g, 2)
                    need(pe, prod_done, g - 1)
                elif k == 1:
                    need(pe, sub_done, g)
                else:
                    need(pe, hid_done, g, k - 1)
                need(pe, zlo_done, g)
                for bank, first, full in ((a_bank, c * 128, ina_full), (b_bank, H + c * 128, inb_full)):
                    cols = slice(first, first + 128)
                    mm(bank[:, 0:n], w_in_hi[:, net, cols], z_hi[:, 0:n], start=True, stop=False)
                    mm(bank[:, 0:n], w_in_hi[:, net, cols], z_lo[:, 0:n], start=False, stop=False)
                    mm(bank[:, 0:n], w_in_lo[:, net, cols], z_hi[:, 0:n], start=False, stop=True)\
                        .then_inc(full.sem, 1)

            def counts(g, tiles, rows):
                need(pe, count_done, g)
                if isinstance(g, int) and g == GROUPS - 1:
                    need(pe, zt_done, g)
                elif not is_class(g):
                    need(pe, pt_done, g + 1, 2)
                else:
                    need(pe, route_step, g, 2)
                for t in range(tiles):
                    last = nc.tensor.transpose(count_bank(g)[0:EXPERTS + 1, t * 128:t * 128 + rows], count[0:rows, t, :],
                                               ident[0:rows, 0:rows])
                last.then_inc(cnt_full.sem, 1)

            def shared_out(g, t, rows, final):
                if t == 0:
                    need(pe, hid_done, g)
                    need(pe, cnt_done, g)
                cols = slice(t * 128, t * 128 + rows)
                dst = shared_bank(g)[0:rows, t * D:(t + 1) * D]
                for c in range(HC):
                    mm(dst, hidden[:, c, cols], w_sout[:, c, :], start=(c == 0), stop=False)
                last = mm(dst, count_t[:, cols], out_bias[:, :], start=False, stop=True)
                if final:
                    last.then_inc(sh_full.sem, 1)

            def expert(g, u, rows):
                t, half = u // 2, u % 2
                if u == 0:
                    need(pe, hlo_done, g)
                    if not (isinstance(g, int) and g >= GROUPS - 2):
                        need(pe, nat_done, g + 2)
                elif u == 1 and not (isinstance(g, int) and g >= GROUPS - 1):
                    need(pe, sub_done, g + 1)
                elif u == 3:
                    need(pe, ysh_done, g)
                elif u >= 4:
                    need(pe, prod_done, g, u - 3)
                if isinstance(g, int) and g == GROUPS:
                    need(pe, prod_done, g - 1)
                dst = expert_bank(u)
                cols = slice(t * 128, t * 128 + rows)
                for c in range(HC):
                    w_hi, w_lo = (w[:, c, half * EG:(half + 1) * EG, :].rearrange("p e d -> p (e d)")
                                  for w in (w_eout_hi, w_eout_lo))
                    h_hi, h_lo = hidden_hi[:, c, cols], hidden_lo[:, c, cols]
                    mm(dst[0:rows, :], h_hi, w_hi, start=(c == 0), stop=False)
                    mm(dst[0:rows, :], h_hi, w_lo, start=False, stop=False)
                    last = mm(dst[0:rows, :], h_lo, w_hi, start=False, stop=(c == HC - 1))
                last.then_inc(e_full.sem, 1)

            def class_scores():
                need(pe, cscore_done, GROUPS - 1)
                need(pe, hT_done, GROUPS - 1)
                for half in range(2):
                    last = nc.tensor.transpose(acc[:, half * 128:(half + 1) * 128],
                                               cls_scores[:, half * 128:(half + 1) * 128], ident)
                last.then_inc(tpe.sem, 1)

            def class_probs():
                pe.wait_ge(tdve.sem, 11)
                for half in range(2):
                    last = nc.tensor.transpose(acc[:, 256 + half * 128:256 + (half + 1) * 128],
                                               tc_prob[:, 2 * half:2 * half + 2, :].rearrange("p b m -> p (b m)"), ident)
                last.then_inc(tpe.sem, 1)

            def class_values():
                pe.wait_ge(tact.sem, 3)
                pe.wait_ge(tdve.sem, 13)
                pe.wait_ge(tpool.sem, 1)
                mm(acc[:, 0:IMAGES], v_cls_rows[:, :], tc_pcc_bd[:, :, :, :].rearrange("p a b c -> p (a b c)"),
                   start=True, stop=False, skip_group_check=True)
                for pair in range(IMAGES // 2):
                    last = mm(acc[:, 2 * pair:2 * pair + 2], tc_pv[:, pair, :], const[:, C_B2:C_B2 + 2],
                              start=False, stop=(pair == IMAGES // 2 - 1), skip_group_check=True)
                last.then_inc(tpe.sem, 1)

            def class_out():
                pe.wait_ge(tact.sem, 4)
                mm(acc[0:IMAGES, 128:256], tc_attn_t[:, :], wo[:, :], start=True, stop=True).then_inc(tpe.sem, 1)

            patch(0, 0, 12)
            pe.wait_ge(w_first.sem, FIRST)
            pe.wait_ge(w_row.sem, ROW)
            pe.wait_ge(hcls_step.sem, 4)
            nc.tensor.transpose(B1[:, 0:128], hn_cls[:, :], ident).then_inc(cpe.sem, 1)
            patch(0, 12, 14)
            pe.wait_ge(cact.sem, 1)
            mm(O[:, 0:128], hn_cls_t[:, :], wq[:, :], start=True, stop=True)
            mm(O[:, 128:256], hn_cls_t[:, :], wk[:, :], start=True, stop=True)
            mm(O[:, 256:384], hn_cls_t[:, :], wv[:, :], start=True, stop=True)
            mm(O[:, 384:512], bv_col[:, 0:1].to_broadcast([128, 128]), wo[:, :], start=True, stop=True)\
                .then_inc(cpe.sem, 1)
            patch(0, 14, 17)
            pe.wait_ge(cdve.sem, 9)
            nc.tensor.transpose(C0[:, 0:128], k_cls[:, :], ident)
            nc.tensor.transpose(C0[:, 128:256], qn_cls[:, :], ident).then_inc(cpe.sem, 1)
            patch(0, 17, NMAIN + 1)
            to_natural(0)
            patch(1, 0, AHEAD)
            normed_t(0)

            def body(g, par):
                nxt, last = has_next(g), has_last(g)

                ahead = 0 if last else AHEAD

                def fill(j0, j1):
                    if nxt and j1 > ahead:
                        patch(g + 1, max(j0, ahead), j1)

                k_proj(g)
                if last and not is_int(g, 1):
                    gates(g - 1, TILES, 128)
                q_proj(g)
                if is_int(g, 1):
                    z_transpose(0)
                k_sums(g)
                v_proj(g)
                if is_int(g, 1):
                    gates(0, TILES, 128)
                    pe.wait_ge(wlo_done.sem, 4)
                if last:
                    ffn_in(g - 1, 0, TOK)
                    ffn_in(g - 1, 1, TOK)
                if not nxt:
                    class_scores()
                q_transpose(g)
                if last:
                    ffn_in(g - 1, 2, TOK)
                    ffn_in(g - 1, 3, TOK)
                fill(0, 1)
                score(g, 0)
                fill(1, 3)
                score(g, 1)
                fill(3, 5)
                prob_transpose(g, 0)
                fill(5, 6)
                prob_v(g, 0)
                score(g, 2)
                fill(6, 9)
                prob_transpose(g, 1)
                fill(9, 10)
                if not nxt:
                    expert(g - 1, 0, 128)
                prob_v(g, 1)
                if not nxt:
                    class_probs()
                score(g, 3)
                fill(10, 13)
                if not nxt:
                    counts(g - 1, TILES, 128)
                prob_transpose(g, 2)
                if nxt and last:
                    counts(g - 1, TILES, 128)
                fill(13, 14)
                if not nxt:
                    shared_out(g - 1, 0, 128, False)
                    shared_out(g - 1, 1, 128, False)
                    shared_out(g - 1, 2, 128, False)
                prob_v(g, 2)
                fill(14, 18)
                prob_transpose(g, 3)
                fill(18, NMAIN + 1)
                if nxt and last:
                    shared_out(g - 1, 0, 128, False)
                    shared_out(g - 1, 1, 128, False)
                elif not nxt:
                    shared_out(g - 1, 3, 128, True)
                    expert(g - 1, 1, 128)
                prob_v(g, 3)
                if nxt:
                    to_natural(g + 1)
                if nxt and last:
                    shared_out(g - 1, 2, 128, False)
                    shared_out(g - 1, 3, 128, True)
                    expert(g - 1, 0, 128)
                elif not nxt:
                    expert(g - 1, 2, 128)
                attn_transpose(g)
                if nxt and last:
                    expert(g - 1, 1, 128)
                out_proj(g)
                if nxt and last:
                    expert(g - 1, 2, 128)
                if nxt:
                    normed_t(g + 1)
                else:
                    class_values()
                if last:
                    expert(g - 1, 3, 128)
                if last:
                    expert(g - 1, 4, 128)
                if not nxt:
                    class_out()
                if nxt and last:
                    expert(g - 1, 5, 128)
                if last:
                    z_transpose(g)
                if not nxt:
                    expert(g - 1, 5, 128)
                if last:
                    expert(g - 1, 6, 128)
                    expert(g - 1, 7, 128)

            pe.wait_ge(cdve.sem, 19)
            groups(pe, body)

            L = GROUPS - 1
            gates(L, TILES, 128)
            for k in range(4):
                ffn_in(L, k, TOK)
            counts(L, TILES, 128)
            for t in range(TILES):
                shared_out(L, t, 128, t == TILES - 1)
            need(pe, z_done, GROUPS, 1)
            nc.tensor.transpose(B1[:, 0:IMAGES], z_nat[0:IMAGES, 0:128], ident[0:IMAGES, 0:IMAGES])\
                .then_inc(zt_full.sem, 1)
            expert(L, 0, 128)
            gates(GROUPS, 1, IMAGES)
            for u in range(1, 4):
                expert(L, u, 128)
            ffn_in(GROUPS, 0, IMAGES)
            ffn_in(GROUPS, 1, IMAGES)
            expert(L, 4, 128)
            expert(L, 5, 128)
            ffn_in(GROUPS, 2, IMAGES)
            ffn_in(GROUPS, 3, IMAGES)
            counts(GROUPS, 1, IMAGES)
            expert(L, 6, 128)
            expert(L, 7, 128)
            shared_out(GROUPS, 0, IMAGES, True)
            expert(GROUPS, 0, IMAGES)
            expert(GROUPS, 1, IMAGES)

        @block.scalar
        def _(act):
            def go(dst, src, func=ACT.Copy, **kw):
                return nc.scalar.activation(dst, src, func, **kw)

            def load_table(g, k, func):
                need(act, table_done, g, k)
                go(table_row[:, :], const[:, 0:1], func).then_inc(table_done.sem, 1)

            def natural(g, par):
                need(act, nat_full, g)
                need(act, h2_done, g - 2)
                go(h_nat[par][:, :], C1[:, :]).then_inc(nat_done.sem, 1)

            def normed_t(g):
                need(act, hnt_full, g)
                go(hn_t[:, :], B1[:, :]).then_inc(hnt_done.sem, 1)

            def k_plain(g):
                need(act, k_full, g)
                go(k_t[:, :], B1[:, :], ACT.Relu, bias=bk_col[:, 0:1]).then_inc(kt_done.sem, 1)

            def q_masked(g):
                need(act, qt_full, g)
                for e in range(2):
                    go(q_mask[:, :, e, :], B1[:, :].rearrange("p (b n) -> p b n", n=NPATCH),
                       scale=const[:, C_PAR + e:C_PAR + e + 1]).then_inc(q_done.sem, 1)

            def v_blocks(g):
                need(act, v_full, g)
                for b2 in range(2):
                    r = slice(64 * b2, 64 * b2 + 64)
                    go(v_bd[r, bass.ds(g * TILES, TILES), :, b2, :], B0[r, :].rearrange("p (a h c) -> p a h c", h=HP, c=32))\
                        .then_inc(v_done.sem, 1)

            def k_blocks(g):
                need(act, k_full, g)
                for hp in range(HP):
                    r = slice(32 * hp, 32 * hp + 32)
                    go(k_bd[r, :, hp, 0:NPATCH], B1[r, :].rearrange("p (b m) -> p b m", m=NPATCH), ACT.Relu,
                       bias=bk_col[r, 0:1])\
                        .then_inc(kbd_done.sem, 1)

            def exps(g, p):
                need(act, sub_done, g, p + 1)
                need(act, pt_full, *((g, p - 1) if p >= 2 else (g - 1, p + 3)))
                need(act, psum_done, *((g, p - 1) if p >= 2 else (g - 1, p + 3)))
                need(act, pcls_done, g - 1, p // 2 + 1)
                go(probs[p % 2][:, :, :].rearrange("p h (b m) -> p h b m", b=2),
                   shift[p % 2][:, :, :, 0:NPATCH].rearrange("p b h m -> p h b m"), ACT.Exp).then_inc(exp_done.sem, 1)
                go(exp_cls[:, p], shift[p % 2][:, :, :, NPATCH].rearrange("p b h -> p h b"), ACT.Exp)\
                    .then_inc(exp_done.sem, 1)

            def probs_out(g, p):
                need(act, pt_full, g, p + 1)
                if p >= 2:
                    need(act, pv_full, g, p - 1)
                go(probs_t[p % 2][:, :], prob_bank(p)[:, :]).then_inc(pt_done.sem, 1)

            def attn_out(g):
                need(act, ot_full, g)
                go(attn_t[:, :], B1[:, :]).then_inc(ot_done.sem, 1)

            def z_out(g, n):
                need(act, zt_full, g)
                need(act, inb_full, g - 1)
                for dst in (z_hi, z_t):
                    go(dst[:, 0:n], z_bank(g)[:, 0:n], ACT.Identity, scale=ln_scale[:, 0:1], bias=ln_bias[:, 0:1])\
                        .then_inc(zt_done.sem, 1)

            def hidden_high(g, c, n):
                need(act, hid_done, g, HC + c + 1)
                if is_class(g):
                    need(act, e_full, g - 1, 2)
                go(hidden_hi[:, c, 0:n], silu[c][:, 0:n]).then_inc(hhi_done.sem, 1)

            def route_exp(g, tiles, rows):
                need(act, shift_done, g)
                go(e_exp[0:rows, 0:2 * tiles, :], e_shift[0:rows, 0:2 * tiles, :], ACT.Exp).then_inc(rexp_done.sem, 1)

            def silus(g, k, n):
                need(act, inb_full if is_class(g) else ina_full, g, k + 1)
                if k >= 2:
                    need(act, hid_done, g, k - 1)
                else:
                    need(act, hlo_done, g - 1, k + 1)
                go(silu[k % 2][:, 0:n], ffn_banks(g, k)[0][:, 0:n], ACT.Silu).then_inc(silu_done.sem, 1)

            def counts_out(g, n):
                need(act, cnt_full, g)
                go(count_t[:, 0:n], count_bank(g)[0:EXPERTS + 1, 0:n]).then_inc(cnt_done.sem, 1)

            for i, (a, b) in enumerate(PIECES):
                act.dma_start(w_patch[:, a:b, :], A["w_patch"][:, a:b, :]).then_inc(w_piece[i].sem, 16)
                if i == 1:
                    for dst, src in first_loads:
                        act.dma_start(dst, src).then_inc(w_first.sem, 16)
                elif i == 3:
                    for dst, src in row_loads:
                        act.dma_start(dst, src).then_inc(w_row.sem, 16)
            act.wait_ge(cpe.sem, 1)
            go(hn_cls_t[:, :], B1[:, 0:128]).then_inc(cact.sem, 1)
            act.wait_ge(cpe.sem, 3)
            go(k_cls_t[:, :], C0[:, 0:1]).then_inc(cact.sem, 1)
            go(qn_cls_t[:, :], C0[:, 128:129]).then_inc(cact.sem, 1)
            act.wait_ge(pool_init.sem, POOL_INIT)
            act.wait_ge(cact.sem, 3)
            for hp in range(HP):
                r = slice(32 * hp, 32 * hp + 32)
                go(k_bd[r, :, hp, NPATCH:SEQ], k_cls_t[r, 0:1].unsqueeze(2).to_broadcast([32, GROUP_IMAGES, 1]))\
                    .then_inc(cact.sem, 1)
            natural(0, 0)
            normed_t(0)

            def body(g, par):
                nxt, last = has_next(g), has_last(g)
                load_table(g, 0, ACT.Silu if last else ACT.Relu)
                k_plain(g)
                k_blocks(g)
                if is_int(g, 1):
                    z_out(0, TOK)
                v_blocks(g)
                if last:
                    silus(g - 1, 0, TOK)
                    silus(g - 1, 1, TOK)
                q_masked(g)
                if last:
                    silus(g - 1, 2, TOK)
                    silus(g - 1, 3, TOK)
                load_table(g, 1, ACT.Exp)
                exps(g, 0)
                if last:
                    hidden_high(g - 1, 0, TOK)
                exps(g, 1)
                probs_out(g, 0)
                if not nxt:
                    act.wait_ge(tdve.sem, 4)
                    go(tc_exp[:, :, :], tc_shift[:, :, :], ACT.Exp).then_inc(tact.sem, 1)
                    go(tc_cc_exp[:, :], tc_cc[:, :], ACT.Exp).then_inc(tact.sem, 1)
                if last:
                    hidden_high(g - 1, 1, TOK)
                    route_exp(g - 1, TILES, 128)
                else:
                    act.wait_ge(w_ffn.sem, FFN)
                    for i in range(2):
                        go(w_in_hi[:, i], w_in_raw[i][:, :]).then_inc(whi_done.sem, 1)
                exps(g, 2)
                probs_out(g, 1)
                if not nxt:
                    act.wait_ge(tpe.sem, 2)
                    go(tc_prob_t[:, :], acc[:, 256:512]).then_inc(tact.sem, 1)
                    counts_out(g - 1, TOK)
                exps(g, 3)
                probs_out(g, 2)
                if nxt and last:
                    counts_out(g - 1, TOK)
                probs_out(g, 3)
                if nxt:
                    natural(g + 1, 1 - par)
                attn_out(g)
                if nxt:
                    normed_t(g + 1)
                else:
                    act.wait_ge(tpe.sem, 3)
                    go(tc_attn_t[:, :], acc[:, 0:IMAGES]).then_inc(tact.sem, 1)
                if last:
                    z_out(g, TOK)
                else:
                    for c in range(HC):
                        go(w_eout_hi[:, c].rearrange("p e d -> p (e d)"), w_eout_raw[c].rearrange("p a b -> p (a b)"))\
                            .then_inc(whi_done.sem, 1)

            groups(act, body)
            L = GROUPS - 1
            load_table(L, 2, ACT.Silu)
            for k in range(4):
                silus(L, k, TOK)
            load_table(L, 3, ACT.Exp)
            counts_out(L, TOK)
            hidden_high(L, 0, TOK)
            hidden_high(L, 1, TOK)
            route_exp(L, TILES, 128)
            z_out(GROUPS, IMAGES)
            route_exp(GROUPS, 1, IMAGES)
            load_table(L, 4, ACT.Silu)
            for k in range(4):
                silus(GROUPS, k, IMAGES)
            hidden_high(GROUPS, 0, IMAGES)
            hidden_high(GROUPS, 1, IMAGES)
            counts_out(GROUPS, IMAGES)

        @block.vector
        def _(dve):
            v = nc.vector

            def bcast(ap, n):
                return ap.unsqueeze(len(ap.shape)).to_broadcast(list(ap.shape) + [n])

            def moments(src, stats, m, var, scale, offset, bn_done, step, var_done, g, tiles, rows):
                r, T = slice(0, rows), slice(0, tiles)
                for t in range(tiles):
                    v.bn_stats(stats[r, t, :], src[r, t * 128:(t + 1) * 128]).then_inc(bn_done.sem, 1)
                need(dve, bn_done, g, tiles)
                v.tensor_tensor(m[r, 1, T], stats[r, T, 1], stats[r, T, 4], ALU.add).then_inc(step.sem, 1)
                v.tensor_tensor(m[r, 2, T], stats[r, T, 1], stats[r, T, 4], ALU.subtract).then_inc(step.sem, 1)
                v.tensor_tensor(m[r, 3, T], stats[r, T, 2], stats[r, T, 5], ALU.add).then_inc(step.sem, 1)
                need(dve, step, g, 2)
                v.tensor_scalar(m[r, 0, T], m[r, 1, T], 0.5, None, ALU.mult).then_inc(step.sem, 1)
                v.scalar_tensor_tensor(m[r, 4, T], m[r, 2, T], D / 4.0, m[r, 2, T], ALU.mult, ALU.mult)\
                    .then_inc(step.sem, 1)
                need(dve, step, g, 5)
                v.tensor_tensor(m[r, 5, T], m[r, 3, T], m[r, 4, T], ALU.add).then_inc(step.sem, 1)
                need(dve, step, g, 6)
                v.tensor_scalar(var[r, T], m[r, 5, T], scale / D, offset, ALU.mult, ALU.add).then_inc(var_done.sem, 1)

            def normalise(dst, src, mv, rstd, done, tiles, rows):
                for t in range(tiles):
                    v.tensor_scalar(dst[0:rows, t * 128:(t + 1) * 128], src[0:rows, t * 128:(t + 1) * 128],
                                    mv[0:rows, 0, t:t + 1], rstd[0:rows, t:t + 1], ALU.subtract, ALU.mult)\
                        .then_inc(done.sem, 1)

            def tokens(g):
                need(dve, acc_full, g)
                v.scalar_tensor_tensor(h_t[:, :].rearrange("p (b n) -> p b n", n=NPATCH),
                                       acc[:, :].rearrange("p (b n) -> p b n", n=NPATCH), tok_b[:, 0:1],
                                       pos_t[:, :].unsqueeze(1).to_broadcast([128, GROUP_IMAGES, NPATCH]),
                                       ALU.add, ALU.mult).then_inc(hT_done.sem, 1)

            def norm1(g, par):
                need(dve, nat_done, g)
                moments(h_nat[par], stats1, mv1, var1, 1.0, LN_EPS, bn1_done, mv1_step, var1_done, g, TILES, 128)

            def norm1_scale(g, par):
                need(dve, rstd1_done, g)
                normalise(hn_nat, h_nat[par], mv1, rstd1, hn_done, TILES, 128)

            def q_add(g):
                need(dve, q_full, g)
                need(dve, qt_full, g - 1)
                v.tensor_tensor(q_nat[:, :].rearrange("p (t d) -> p t d", d=D),
                                B0[:, :].rearrange("p (t d) -> p t d", d=D),
                                bq_row[:, :].unsqueeze(1).to_broadcast([128, TILES, D]), ALU.add)\
                    .then_inc(qraw_done.sem, 1)

            def q_norm(g):
                need(dve, ks_full, g)
                sums = O[:, 0:TILES * 16].rearrange("p (t n) -> p t n", n=16)
                v.tensor_scalar(q_sum_eps[:, :, :], sums[:, :, 0:HEADS], ATTN_EPS, None, ALU.add).then_inc(ks_step.sem, 1)
                v.tensor_copy(cls_scores[:, bass.ds(g * (TILES * HEADS), TILES * HEADS)]
                              .rearrange("p (t n) -> p t n", n=HEADS), sums[:, :, HEADS:16]).then_inc(cscore_done.sem, 1)
                need(dve, ks_step, g, 1)
                v.reciprocal(q_rec[:, :, :], q_sum_eps[:, :, :]).then_inc(ks_step.sem, 1)
                need(dve, ks_step, g, 2)
                need(dve, qraw_done, g)
                v.scalar_tensor_tensor(q_nat[:, :].rearrange("p (h d) -> p h d", d=DH),
                                       q_nat[:, :].rearrange("p (h d) -> p h d", d=DH), 0.0,
                                       bcast(q_rec[:, :, :].rearrange("p t h -> p (t h)"), DH), ALU.max, ALU.mult)\
                    .then_inc(qn_done.sem, 1)

            def row_maxes(g, p):
                need(dve, s_full, g, p + 1)
                s = scores[:, :, 0:HP * SEQ].rearrange("p b (h m) -> p b h m", m=SEQ)
                v.tensor_reduce(row_max[p % 2][:, :, :], s, AX.X, ALU.max).then_inc(max_done.sem, 1)
                need(dve, max_done, g, p + 1)
                need(dve, exp_done, *((g, 2 * (p - 1)) if p >= 2 else (g - 1, 2 * (p + 3))))
                v.tensor_tensor(shift[p % 2][:, :, :, :], s, bcast(row_max[p % 2][:, :, :], SEQ), ALU.subtract)\
                    .then_inc(sub_done.sem, 1)

            def row_sums(g, p):
                need(dve, exp_done, g, 2 * p + 2)
                v.tensor_reduce(patch_sum[:, p], probs[p % 2][:, :, :].rearrange("p h (b m) -> p h b m", b=2), AX.X,
                                ALU.add).then_inc(psum_done.sem, 1)
                if p % 2:
                    half = p // 2
                    pair = slice(2 * half, 2 * half + 2)
                    need(dve, psum_done, g, p + 1)
                    v.tensor_tensor(row_sum[:, pair], patch_sum[:, pair], exp_cls[:, pair], ALU.add)\
                        .then_inc(sum_done.sem, 1)
                    need(dve, sum_done, g, half + 1)
                    need(dve, pcls_done, g - 1, half + 1)
                    v.reciprocal(row_rec[:, pair], row_sum[:, pair])\
                        .then_inc(rec_done.sem, 1)

            def attn_scale(g, half):
                need(dve, pv_full, g, 2 * half + 2)
                need(dve, rec_done, g, half + 1)
                o = O[:, :].rearrange("p (a b e d) -> p a b e d", a=8, b=2, e=2)
                for e in range(2):
                    r = slice(64 * e, 64 * e + 64)
                    rec = row_rec[r, 2 * half:2 * half + 2].rearrange("p a h b -> p (a h) b")
                    v.tensor_tensor(attn_patch[half][r], o[r, :, :, e, :], bcast(rec, DH), ALU.mult)\
                        .then_inc(o1_done.sem, 1)

            def attn_sum(g, half):
                need(dve, acls_done, g, 2 * half + 2)
                need(dve, o1_done, g, 2 * half + 2)
                if half == 0:
                    need(dve, ot_full, g - 1)
                cls = attn_cls[half][:, :, :, :, :].rearrange("p a h b d -> p (a h) b d")
                dst = attn_nat[:, 2 * half:2 * half + 2].rearrange("p a h e d -> p (a h) e d")
                for b2 in range(2):
                    for e in range(2):
                        o, r = slice(64 * b2, 64 * b2 + 64), slice(64 * e, 64 * e + 64)
                        v.tensor_tensor(dst[o, :, e, :], attn_patch[half][r, :, b2, :], cls[r, :, b2, :], ALU.add)\
                            .then_inc(attn_done.sem, 1)

            def residual(g, par):
                need(dve, y_full, g)
                need(dve, hbo_done, g)
                v.tensor_tensor(h2[par][:, :], B0[:, :], h_nat[par][:, :], ALU.add).then_inc(h2_done.sem, 1)

            def norm2(g, src, tiles, rows):
                need(dve, h2_done, g)
                moments(src, stats2, mv2, var2, 1.0 + LN_EPS, LN_EPS * LN_EPS, bn2_done, mv2_step, var2_done, g, tiles,
                        rows)

            def norm2_scale(g, src, tiles, rows):
                need(dve, rstd2_done, g)
                normalise(z_nat, src, mv2, rstd2, z_done, tiles, rows)

            def logits(g, tiles, rows):
                r, T, S = slice(0, rows), tiles, 2 * tiles
                gates_ps = gate_bank(g)[r, 0:T * NGATE].rearrange("p (t n) -> p t n", n=NGATE)
                gb = gate_b[r, :].unsqueeze(1).to_broadcast([rows, T, NGATE])
                need(dve, g_full, g)
                v.tensor_tensor(g_logit[r, 0:T], gates_ps[:, :, 0:2], gb[:, :, 0:2], ALU.add).then_inc(route_step.sem, 1)
                v.tensor_tensor(e_logit[r, 0:S].rearrange("p (t a) e -> p t (a e)", a=2), gates_ps[:, :, 2:NGATE],
                                gb[:, :, 2:NGATE], ALU.add).then_inc(route_step.sem, 1)

            def choose(g, tiles, rows):
                def chained(ins):
                    nonlocal n
                    ins.then_inc(route_step.sem, 1)
                    n += 1
                    need(dve, route_step, g, n)

                n = 2
                r, T, S = slice(0, rows), tiles, 2 * tiles
                need(dve, route_step, g, n)
                chained(v.tensor_tensor(g_sel[r, 0:T, 1], g_logit[r, 0:T, 1], g_logit[r, 0:T, 0], ALU.is_gt))
                chained(v.tensor_scalar(g_sel[r, 0:T, 0], g_sel[r, 0:T, 1], -1.0, 1.0, ALU.mult, ALU.add))
                chained(v.tensor_reduce(e_max[r, 0:S], e_logit[r, 0:S], AX.X, ALU.max))
                need(dve, rexp_done, g - 1)
                v.tensor_tensor(e_shift[r, 0:S], e_logit[r, 0:S], bcast(e_max[r, 0:S], EG), ALU.subtract)\
                    .then_inc(shift_done.sem, 1)
                lj = e_logit[r, 0:S].unsqueeze(2).to_broadcast([rows, S, EG, EG])
                ge = e_ge[r, 0:S].rearrange("p s (i j) -> p s i j", j=EG)
                chained(v.tensor_tensor(ge, lj, bcast(e_logit[r, 0:S], EG), ALU.is_ge))
                chained(v.tensor_tensor(e_ge[r, 0:S], e_ge[r, 0:S],
                                        const[r, C_TRI:C_TRI + 16].unsqueeze(1).to_broadcast([rows, S, 16]), ALU.mult))
                chained(v.tensor_reduce(e_row[r, 0:S], ge, AX.X, ALU.add))
                chained(v.tensor_reduce(e_col[r, 0:S], ge.rearrange("p s i j -> p s j i"), AX.X, ALU.add))
                chained(v.tensor_tensor(e_top[r, 0:S], e_row[r, 0:S], e_col[r, 0:S], ALU.subtract))
                chained(v.tensor_tensor(e_row[r, 0:S], e_top[r, 0:S],
                                        const[r, C_THR:C_THR + EG].unsqueeze(1).to_broadcast([rows, S, EG]), ALU.is_lt))
                cnt = count[r, 0:T, 0:EXPERTS].rearrange("p t (a e) -> p t a e", e=EG)
                need(dve, cnt_full, g - 1)
                v.tensor_tensor(cnt, e_row[r, 0:S].rearrange("p (t a) e -> p t a e", a=2), bcast(g_sel[r, 0:T], EG),
                                ALU.mult).then_inc(count_done.sem, 1)

            def weights(g, tiles, rows):
                def chained(ins):
                    nonlocal n
                    ins.then_inc(route_step.sem, 1)
                    n += 1
                    need(dve, route_step, g, n)

                n = 11
                r, T, S = slice(0, rows), tiles, 2 * tiles
                need(dve, count_done, g)
                need(dve, rexp_done, g)
                ex = e_exp[r, 0:S].rearrange("p (t a) e -> p t (a e)", a=2)
                chained(v.tensor_tensor(e_keep[r, 0:T], ex, count[r, 0:T, 0:EXPERTS], ALU.mult))
                chained(v.tensor_tensor(e_group[r, 0:T].rearrange("p t (a e) -> p t a e", e=EG),
                                        e_exp[r, 0:S].rearrange("p (t a) e -> p t a e", a=2), bcast(g_sel[r, 0:T], EG),
                                        ALU.mult))
                chained(v.tensor_reduce(e_den[r, 0, 0:T], e_keep[r, 0:T], AX.X, ALU.add))
                chained(v.tensor_reduce(e_den[r, 1, 0:T], e_group[r, 0:T], AX.X, ALU.add))
                chained(v.scalar_tensor_tensor(e_den[r, 2, 0:T], e_den[r, 1, 0:T], 1e-8, e_den[r, 0, 0:T],
                                               ALU.mult, ALU.add))
                chained(v.reciprocal(e_den[r, 3, 0:T], e_den[r, 2, 0:T]))
                v.tensor_tensor(comb[r, 0:T], e_keep[r, 0:T], bcast(e_den[r, 3, 0:T], EXPERTS), ALU.mult)\
                    .then_inc(comb_done.sem, 1)
                assert n == route_step.per, n

            def hidden_mul(g, k, n):
                net, c = k // 2, k % 2
                need(dve, silu_done, g, k + 1)
                need(dve, inb_full, g, k + 1)
                dst = silu[c] if net else hidden[:, c]
                v.tensor_tensor(dst[:, 0:n], silu[k % 2][:, 0:n], ffn_banks(g, k)[1][:, 0:n], ALU.mult)\
                    .then_inc(hid_done.sem, 1)

            def shared_add(g, src, tiles, rows):
                need(dve, sh_full, g)
                if not is_class(g):
                    need(dve, stored, g - 1)
                dst = y_cls if is_class(g) else y_out
                v.tensor_tensor(dst[0:rows, 0:tiles * D], shared_bank(g)[0:rows, 0:tiles * D],
                                src[0:rows, 0:tiles * D], ALU.add).then_inc(ysh_done.sem, 1)

            def weigh(g, u, rows):
                t, half = u // 2, u % 2
                need(dve, e_full, g, u + 1)
                if u == 0:
                    need(dve, comb_done, g)
                if half == 0:
                    if t >= 2:
                        need(dve, tree_done, g, t - 1)
                    else:
                        need(dve, tree_done, g - 1, t + 3)
                src = expert_bank(u)
                v.tensor_tensor(prod[t % 2][0:rows, half, :].rearrange("p (e d) -> p e d", d=D),
                                src[0:rows, :].rearrange("p (e d) -> p e d", d=D),
                                bcast(comb[0:rows, t, half * EG:(half + 1) * EG], D), ALU.mult).then_inc(prod_done.sem, 1)

            def output(g, tiles, rows):
                need(dve, ysh_done, g)
                need(dve, tree_done, g, tiles)
                y = y_cls if is_class(g) else y_out
                v.tensor_tensor(y[0:rows, 0:tiles * D], y[0:rows, 0:tiles * D],
                                (routed_cls if is_class(g) else routed)[0:rows, 0:tiles].rearrange("p t d -> p (t d)"), ALU.add).then_inc(yout_done.sem, 1)

            dve.wait_ge(w_first.sem, FIRST)
            dve.wait_ge(w_row.sem, ROW)
            v.tensor_tensor(h_cls[:, :], cls_row[:, :], pos0_row[:, :], ALU.mult).then_inc(hcls_step.sem, 1)
            v.tensor_copy(k_sel[:, 0:HEADS], const[:, C_HEAD:C_HEAD + HEADS]).then_inc(cdve.sem, 1)
            dve.wait_ge(hcls_step.sem, 1)
            v.bn_stats(cls_stats[:, :], h_cls[:, :]).then_inc(hcls_step.sem, 1)
            dve.wait_ge(hcls_step.sem, 2)
            v.bn_aggr(cls_mv[:, :], cls_stats[:, :]).then_inc(hcls_step.sem, 1)
            dve.wait_ge(cpow_step.sem, 2)
            dve.wait_ge(hcls_step.sem, 3)
            v.tensor_scalar(hn_cls[:, :], h_cls[:, :], cls_mv[:, 0:1], cls_rstd[:, 0:1], ALU.subtract, ALU.mult)\
                .then_inc(hcls_step.sem, 1)
            dve.wait_ge(cpe.sem, 2)
            v.tensor_tensor(q_cls_raw[:, :], O[:, 0:128], bq_row[:, :], ALU.add).then_inc(cdve.sem, 1)
            v.tensor_tensor(k_cls_raw[:, :], O[:, 128:256], bk_row[:, :], ALU.add).then_inc(cdve.sem, 1)
            dve.wait_ge(cdve.sem, 3)
            v.tensor_scalar(q_cls[:, :], q_cls_raw[:, :], 0.0, None, ALU.max).then_inc(cdve.sem, 1)
            v.tensor_scalar(k_cls[:, :], k_cls_raw[:, :], 0.0, None, ALU.max).then_inc(cdve.sem, 1)
            dve.wait_ge(cdve.sem, 5)
            kv = k_cls[:, :].rearrange("p (h d) -> p h d", d=DH)
            v.tensor_reduce(k_cls_sum[:, 0:8], kv, AX.X, ALU.add).then_inc(cdve.sem, 1)
            dve.wait_ge(cdve.sem, 6)
            v.tensor_scalar(k_cls_sum[:, 8:16], k_cls_sum[:, 0:8], ATTN_EPS, None, ALU.add).then_inc(cdve.sem, 1)
            dve.wait_ge(cdve.sem, 7)
            v.reciprocal(k_cls_sum[:, 16:24], k_cls_sum[:, 8:16]).then_inc(cdve.sem, 1)
            dve.wait_ge(cdve.sem, 8)
            v.tensor_tensor(qn_cls[:, :].rearrange("p (h d) -> p h d", d=DH),
                            q_cls[:, :].rearrange("p (h d) -> p h d", d=DH), bcast(k_cls_sum[:, 16:24], DH),
                            ALU.mult).then_inc(cdve.sem, 1)
            v.tensor_copy(v_cls[:, :], O[:, 256:384]).then_inc(cdve.sem, 1)
            v.tensor_tensor(bo2[:, :], O[:, 384:512], bo_row[:, :], ALU.add).then_inc(cdve.sem, 1)
            dve.wait_ge(cdve.sem, 11)
            for e in range(2):
                r = slice(64 * e, 64 * e + 64)
                v.tensor_copy(v_cls_hp[r], v_cls[r].rearrange("p (h e d) -> p h e d", e=2, d=DH)[:, :, e, :])\
                    .then_inc(cdve.sem, 1)
            v.tensor_tensor(cc_mul[:, :], qn_cls[:, :], k_cls[:, :], ALU.mult).then_inc(cdve.sem, 1)
            v.tensor_tensor(v_cls_rows[:, :], v_cls[:, :], const[:, C_HMASK:C_HMASK + 128], ALU.mult)\
                .then_inc(cdve.sem, 1)
            v.tensor_tensor(h_cls_bo[:, :], h_cls[:, :], bo2[:, :], ALU.add).then_inc(cdve.sem, 1)
            dve.wait_ge(cdve.sem, 16)
            v.tensor_reduce(cc_row[:, :], cc_mul[:, :].rearrange("p (h d) -> p h d", d=DH), AX.X, ALU.add)\
                .then_inc(cdve.sem, 1)
            dve.wait_ge(cdve.sem, 17)
            v.tensor_tensor(cc_pick[:, :], cc_row[:, :], const[:, C_HROW:C_HROW + 8], ALU.mult).then_inc(cdve.sem, 1)
            dve.wait_ge(cdve.sem, 18)
            dve.wait_ge(cact.sem, 3)
            v.tensor_scalar(k_sel[:, HEADS:16], const[:, C_HEAD:C_HEAD + HEADS], qn_cls_t[:, 0:1], None, ALU.mult)\
                .then_inc(cdve.sem, 1)
            v.tensor_reduce(cc_col[:, :], cc_pick[:, :], AX.X, ALU.add).then_inc(cdve.sem, 1)
            tokens(0)
            norm1(0, 0)
            norm1_scale(0, 0)

            def class_max():
                dve.wait_ge(tpe.sem, 1)
                s = acc[:, 0:256].rearrange("p (a m) -> p a m", m=NPATCH)
                v.tensor_reduce(tc_max0[:, :], s, AX.X, ALU.max).then_inc(tdve.sem, 1)
                dve.wait_ge(tdve.sem, 1)
                v.tensor_scalar(tc_max[:, :], tc_max0[:, :], cc_col[:, 0:1], None, ALU.max).then_inc(tdve.sem, 1)
                dve.wait_ge(tdve.sem, 2)
                v.tensor_tensor(tc_shift[:, :, :], s, bcast(tc_max[:, :], NPATCH), ALU.subtract)\
                    .then_inc(tdve.sem, 1)
                v.tensor_scalar(tc_cc[:, :], tc_max[:, :], -1.0, cc_col[:, 0:1], ALU.mult, ALU.add)\
                    .then_inc(tdve.sem, 1)

            def class_softmax():
                dve.wait_ge(tact.sem, 2)
                v.tensor_reduce(tc_sum[:, 0, :], tc_exp[:, :, :], AX.X, ALU.add).then_inc(tdve.sem, 1)
                dve.wait_ge(tdve.sem, 5)
                v.tensor_tensor(tc_sum[:, 1, :], tc_sum[:, 0, :], tc_cc_exp[:, :], ALU.add).then_inc(tdve.sem, 1)
                dve.wait_ge(tdve.sem, 6)
                v.reciprocal(tc_sum[:, 2, :], tc_sum[:, 1, :]).then_inc(tdve.sem, 1)
                dve.wait_ge(tdve.sem, 7)
                v.tensor_tensor(tc_pcc[:, :], tc_cc_exp[:, :], tc_sum[:, 2, :], ALU.mult).then_inc(tdve.sem, 1)
                dve.wait_ge(tdve.sem, 8)
                for half in range(2):
                    v.tensor_tensor(tc_pcc_bd[:, half],
                                    tc_pcc[:, 2 * half:2 * half + 2].unsqueeze(1).to_broadcast([128, 16, 2]),
                                    bcast(const[:, C_PMASK:C_PMASK + 16], 2), ALU.mult).then_inc(tdve.sem, 1)
                v.tensor_tensor(tc_prob[:, :, :], tc_exp[:, :, :], bcast(tc_sum[:, 2, :], NPATCH), ALU.mult)\
                    .then_inc(tdve.sem, 1)

            def class_weigh(half):
                dve.wait_ge(tact.sem, 3)
                pairs = slice(16 * half, 16 * half + 16)
                v.tensor_tensor(tc_pv[0:64, pairs, :].rearrange("p a (h e d) -> p (a h) e d", e=2, d=DH),
                                v_bd[0:64, pairs, :, 0, :].rearrange("p a h (e d) -> p (a h) e d", e=2),
                                bcast(tc_prob_t[0:64, 128 * half:128 * half + 128]
                                      .rearrange("p (a e) -> p a e", e=2), DH), ALU.mult).then_inc(tdve.sem, 1)

            def body(g, par):
                nxt, last = has_next(g), has_last(g)
                if last and not is_int(g, 1):
                    logits(g - 1, TILES, 128)
                q_add(g)
                q_norm(g)
                if is_int(g, 1):
                    logits(0, TILES, 128)
                if last:
                    hidden_mul(g - 1, 0, TOK)
                    hidden_mul(g - 1, 1, TOK)
                if last and has_last(g - 1):
                    output(g - 2, TILES, 128)
                if last:
                    hidden_mul(g - 1, 2, TOK)
                    hidden_mul(g - 1, 3, TOK)
                row_maxes(g, 0)
                row_maxes(g, 1)
                if not nxt:
                    class_max()
                row_sums(g, 0)
                if last:
                    choose(g - 1, TILES, 128)
                row_maxes(g, 2)
                row_sums(g, 1)
                if not nxt:
                    class_softmax()
                attn_scale(g, 0)
                row_maxes(g, 3)
                if last:
                    weights(g - 1, TILES, 128)
                row_sums(g, 2)
                attn_sum(g, 0)
                row_sums(g, 3)
                if nxt:
                    tokens(g + 1)
                else:
                    class_weigh(0)
                attn_scale(g, 1)
                attn_sum(g, 1)
                if nxt:
                    norm1(g + 1, 1 - par)
                else:
                    class_weigh(1)
                if last:
                    shared_add(g - 1, h2[1 - par], TILES, 128)
                if nxt:
                    norm1_scale(g + 1, 1 - par)
                if last:
                    weigh(g - 1, 0, 128)
                residual(g, par)
                norm2(g, h2[par], TILES, 128)
                if last:
                    weigh(g - 1, 1, 128)
                norm2_scale(g, h2[par], TILES, 128)
                if last:
                    for u in range(2, 2 * TILES):
                        weigh(g - 1, u, 128)

            groups(dve, body)

            L = GROUPS - 1
            logits(L, TILES, 128)
            choose(L, TILES, 128)
            hidden_mul(L, 0, TOK)
            hidden_mul(L, 1, TOK)
            dve.wait_ge(tpe.sem, 4)
            v.tensor_tensor(h2[0][0:IMAGES, 0:D], acc[0:IMAGES, 128:256], h_cls_bo[0:IMAGES, :], ALU.add)\
                .then_inc(h2_done.sem, 1)
            hidden_mul(L, 2, TOK)
            hidden_mul(L, 3, TOK)
            norm2(GROUPS, h2[0], 1, IMAGES)
            norm2_scale(GROUPS, h2[0], 1, IMAGES)
            weights(L, TILES, 128)
            output(L - 1, TILES, 128)
            shared_add(L, h2[1], TILES, 128)
            weigh(L, 0, 128)
            weigh(L, 1, 128)
            logits(GROUPS, 1, IMAGES)
            choose(GROUPS, 1, IMAGES)
            weigh(L, 2, 128)
            weigh(L, 3, 128)
            weights(GROUPS, 1, IMAGES)
            hidden_mul(GROUPS, 0, IMAGES)
            hidden_mul(GROUPS, 1, IMAGES)
            weigh(L, 4, 128)
            hidden_mul(GROUPS, 2, IMAGES)
            hidden_mul(GROUPS, 3, IMAGES)
            weigh(L, 5, 128)
            weigh(L, 6, 128)
            weigh(L, 7, 128)
            shared_add(GROUPS, h2[0], 1, IMAGES)
            weigh(GROUPS, 0, IMAGES)
            weigh(GROUPS, 1, IMAGES)
            output(L, TILES, 128)
            output(GROUPS, 1, IMAGES)

        @block.gpsimd
        def _(pool):
            q = nc.gpsimd

            def norm_scale1(g):
                need(pool, var1_done, g)
                q.tensor_tensor(rstd1[:, :], var1[:, :], neg_half[:, :], ALU.pow).then_inc(rstd1_done.sem, 1)

            def norm_scale2(g, tiles, rows):
                need(pool, var2_done, g)
                q.tensor_tensor(rstd2[0:rows, 0:tiles], var2[0:rows, 0:tiles], neg_half[0:rows, 0:tiles], ALU.pow)\
                    .then_inc(rstd2_done.sem, 1)

            def bias_residual(g, par):
                need(pool, nat_done, g)
                need(pool, hn_done, g)
                q.tensor_tensor(h_nat[par][:, :].rearrange("p (t d) -> p t d", d=D),
                                h_nat[par][:, :].rearrange("p (t d) -> p t d", d=D),
                                bo2[:, :].unsqueeze(1).to_broadcast([128, TILES, D]), ALU.add).then_inc(hbo_done.sem, 1)

            def class_value(g, half):
                need(pool, rec_done, g, half + 1)
                need(pool, attn_done, g - 1, 4 * half + 4)
                pair = slice(2 * half, 2 * half + 2)
                q.tensor_tensor(p_cls[half][:, :, :, :], exp_cls[:, pair],
                                row_rec[:, pair], ALU.mult).then_inc(pcls_done.sem, 1)
                need(pool, pcls_done, g, half + 1)
                for a in range(2):
                    q.tensor_tensor(attn_cls[half][:, a],
                                    p_cls[half][:, a].unsqueeze(3).to_broadcast([128, HP, 2, DH]),
                                    v_cls_hp[:, :, :].unsqueeze(2).to_broadcast([128, HP, 2, DH]), ALU.mult)\
                        .then_inc(acls_done.sem, 1)

            def class_weigh():
                need(pool, acls_done, GROUPS - 1, 2)
                pool.wait_ge(tact.sem, 3)
                q.tensor_tensor(tc_pv[64:128, :, :].rearrange("p a (h e d) -> p (a h) e d", e=2, d=DH),
                                v_bd[64:128, :, :, 1, :].rearrange("p a h (e d) -> p (a h) e d", e=2),
                                tc_prob_t[64:128, :].rearrange("p (a e) -> p a e", e=2).unsqueeze(3)
                                .to_broadcast([64, 128, 2, DH]), ALU.mult).then_inc(tpool.sem, 1)
                pool.wait_ge(tpool.sem, 1)

            def weights_low():
                for i in range(2):
                    pool.wait_ge(whi_done.sem, i + 1)
                    q.tensor_tensor(w_in_lo[:, i], w_in_raw[i][:, :], w_in_hi[:, i].bitcast(F32), ALU.subtract)\
                        .then_inc(wlo_done.sem, 1)
                for c in range(HC):
                    pool.wait_ge(whi_done.sem, 3 + c)
                    q.tensor_tensor(w_eout_lo[:, c].rearrange("p e d -> p (e d)"),
                                    w_eout_raw[c].rearrange("p a b -> p (a b)"),
                                    w_eout_hi[:, c].rearrange("p e d -> p (e d)").bitcast(F32), ALU.subtract)\
                        .then_inc(wlo_done.sem, 1)

            def z_low(g, n):
                need(pool, zt_done, g)
                need(pool, inb_full, g - 1)
                q.tensor_tensor(z_lo[:, 0:n], z_t[:, 0:n], z_hi[:, 0:n].bitcast(F32), ALU.subtract)\
                    .then_inc(zlo_done.sem, 1)

            def hidden_low(g, c, n):
                need(pool, hhi_done, g, c + 1)
                q.tensor_tensor(hidden_lo[:, c, 0:n], silu[c][:, 0:n],
                                hidden_hi[:, c, 0:n].bitcast(F32), ALU.subtract).then_inc(hlo_done.sem, 1)

            def expert_sum(g, t, rows):
                need(pool, prod_done, g, 2 * t + 2)
                r, p = slice(0, rows), prod[t % 2]
                q.tensor_tensor(p[r, 0, :], p[r, 0, :], p[r, 1, :], ALU.add).then_inc(tree1_done.sem, 1)
                need(pool, tree1_done, g, t + 1)
                q.tensor_tensor(p[r, 0, 0:2 * D], p[r, 0, 0:2 * D], p[r, 0, 2 * D:4 * D], ALU.add)\
                    .then_inc(tree2_done.sem, 1)
                need(pool, tree2_done, g, t + 1)
                if t == 0 and not is_class(g):
                    need(pool, yout_done, g - 1)
                q.tensor_tensor((routed_cls if is_class(g) else routed)[r, t, :], p[r, 0, 0:D], p[r, 0, D:2 * D], ALU.add)\
                    .then_inc(tree_done.sem, 1)

            q.memset(neg_half[:, :], -0.5).then_inc(pool_init.sem, 1)
            q.memset(k_bd[:, :, :, :], 0.0).then_inc(pool_init.sem, 1)
            q.memset(v_bd[:, :, :, :, :], 0.0).then_inc(pool_init.sem, 1)
            q.memset(count[:, :, :], 1.0).then_inc(pool_init.sem, 1)
            pool.wait_ge(pool_init.sem, POOL_INIT)
            pool.wait_ge(hcls_step.sem, 3)
            q.tensor_scalar(cls_var[:, :], cls_mv[:, 1:2], LN_EPS, None, ALU.add).then_inc(cpow_step.sem, 1)
            pool.wait_ge(cpow_step.sem, 1)
            q.tensor_tensor(cls_rstd[:, :], cls_var[:, :], neg_half[:, 0:1], ALU.pow).then_inc(cpow_step.sem, 1)
            norm_scale1(0)
            pool.wait_ge(cdve.sem, 16)

            def body(g, par):
                nxt, last = has_next(g), has_last(g)
                bias_residual(g, par)
                if last:
                    hidden_low(g - 1, 0, TOK)
                    hidden_low(g - 1, 1, TOK)
                class_value(g, 0)
                if not nxt:
                    class_weigh()
                class_value(g, 1)
                if nxt:
                    norm_scale1(g + 1)
                norm_scale2(g, TILES, 128)
                if last:
                    for t in range(TILES - 1):
                        expert_sum(g - 1, t, 128)
                else:
                    weights_low()
                z_low(g, TOK)
                if last:
                    expert_sum(g - 1, TILES - 1, 128)

            groups(pool, body)
            L = GROUPS - 1
            norm_scale2(GROUPS, 1, IMAGES)
            hidden_low(L, 0, TOK)
            hidden_low(L, 1, TOK)
            z_low(GROUPS, IMAGES)
            expert_sum(L, 0, 128)
            expert_sum(L, 1, 128)
            hidden_low(GROUPS, 0, IMAGES)
            hidden_low(GROUPS, 1, IMAGES)
            expert_sum(L, 2, 128)
            expert_sum(L, 3, 128)
            expert_sum(GROUPS, 0, IMAGES)


OUT_SHAPE = (IMAGES, SEQ, D)


def kernel(x, L0_tok_W, L0_tok_b, L0_tok_class_token, L0_tok_pos_embed, L0_attn_Wq, L0_attn_bq, L0_attn_Wk,
           L0_attn_bk, L0_attn_Wv, L0_attn_bv, L0_attn_Wo, L0_attn_bo, L0_ffn_ln_scale, L0_ffn_ln_bias,
           L0_ffn_shared_in_w, L0_ffn_shared_out_w, L0_ffn_shared_out_b, L0_ffn_expert_in_w,
           L0_ffn_expert_out_weight, L0_ffn_expert_out_bias, L0_ffn_group_gate_w, L0_ffn_expert_gate_w,
           L0_ffn_group_bias, L0_ffn_expert_bias):
    import concourse.bacc as bacc
    from concourse.bass_utils import run_bass_kernel_spmd

    xg = np.asarray(x).reshape(GROUPS, GROUP_IMAGES, CHANNELS, GRID, PATCH, GRID, PATCH)
    xg = xg.transpose(0, 2, 4, 6, 1, 3, 5).reshape(GROUPS, IN_D, TOK)
    wp = np.asarray(L0_tok_W).T
    main = NMAIN * 128
    pos = np.asarray(L0_tok_pos_embed)

    def t(a):
        return np.asarray(a).T

    def col(a):
        return np.asarray(a).reshape(-1, 1)

    def row(a):
        return np.asarray(a).reshape(1, -1)

    layouts = {
        "x_main": xg[:, :main].reshape(GROUPS, NMAIN, 128, TOK).transpose(0, 2, 1, 3),
        "x_tail": xg[:, main:],
        "w_patch": wp[:main].reshape(NMAIN, 128, D).transpose(1, 0, 2),
        "w_patch_tail": wp[main:],
        "w_attn": np.stack([t(L0_attn_Wq), t(L0_attn_Wk), t(L0_attn_Wv), t(L0_attn_Wo)], 1),
        "rows": np.concatenate([row(L0_attn_bk), row(L0_attn_bo), row(L0_tok_class_token), pos[0:1]], 1),
        "bq_row": row(L0_attn_bq),
        "w_in": np.stack([t(L0_ffn_shared_in_w), t(L0_ffn_expert_in_w)], 1),
        "w_gate": np.concatenate([t(L0_ffn_group_gate_w), t(L0_ffn_expert_gate_w)], 1),
        "gate_b": np.concatenate([row(L0_ffn_group_bias), row(L0_ffn_expert_bias)], 1),
        "w_sout": t(L0_ffn_shared_out_w).reshape(HC, 128, D).transpose(1, 0, 2),
        "w_eout": np.asarray(L0_ffn_expert_out_weight).transpose(2, 0, 1).reshape(HC, 128, EXPERTS, D)
                    .transpose(1, 0, 2, 3),
        "out_bias": np.concatenate([L0_ffn_expert_out_bias, row(L0_ffn_shared_out_b)], 0),
        "const": np.concatenate([shape_constants(), pos[1:].T, col(L0_tok_b), col(L0_attn_bk), col(L0_attn_bv),
                                 col(L0_ffn_ln_scale), col(L0_ffn_ln_bias)], 1),
    }
    nc = bacc.Bacc("TRN2", target_bir_lowering=False, num_devices=1)
    arrays, A = {}, {}
    for name, a in layouts.items():
        a = np.ascontiguousarray(a)
        arrays[f"in_{name}"] = a
        A[name] = nc.dram_tensor(f"in_{name}", a.shape, mybir.dt.from_np(a.dtype), kind="ExternalInput").ap()
    out = nc.dram_tensor("out_tokens", OUT_SHAPE, F32, kind="ExternalOutput").ap()
    vit_tower(nc, A, out)
    r = run_bass_kernel_spmd(nc, [arrays], core_ids=[0])
    return r.results[0]["out_tokens"]
```
